# Optimizing a Trainium2 kernel written in Bass

```python
import numpy as np
import jax
import jax.numpy as jnp

def _softmax(x, axis=-1):
    return jax.nn.softmax(x, axis=axis)

def _gelu(x):
    return jax.nn.gelu(x, approximate=True)

def _silu(x):
    return jax.nn.silu(x)

def _sigmoid(x):
    return jax.nn.sigmoid(x)

def _layernorm(x, axis=-1, eps=1e-05):
    m = jnp.mean(x, axis=axis, keepdims=True)
    v = jnp.var(x, axis=axis, keepdims=True)
    return (x - m) / jnp.sqrt(v + eps)

def _scatter_add(tgt, idx, src, axis=0):
    return tgt.at[idx].add(src)

def _segment_sum(src, seg, n):
    return jax.ops.segment_sum(src, seg, n)
kernel_name = 'mk_gnn_ffn_d1_gnn_r8_986522'

def setup_inputs(seed: int=0):
    np.random.seed(seed)
    _w = jnp.asarray

    def _rec_inputs():
        import jax
        import jax.numpy as jnp
        _gk = jax.random.key(seed)
        x = -0.0003713 + 1 * jax.random.normal(jax.random.fold_in(_gk, 1), (6250, 256), jnp.float32)
        src = jax.random.randint(jax.random.fold_in(_gk, 2), (200000,), 0, 6250, jnp.int32)
        dst = jax.random.randint(jax.random.fold_in(_gk, 3), (200000,), 0, 6250, jnp.int32)
        _o = jnp.argsort(dst, stable=True)
        src = src[_o]
        dst = dst[_o]
        edge_type_8 = jax.random.randint(jax.random.fold_in(_gk, 12), (200000,), 0, 8, jnp.int32)
        return (x, src, dst, edge_type_8)
    x, src, dst, edge_type_8 = _rec_inputs()

    def _L0_gnn_setup():
        import jax, jax.numpy as jnp
        import numpy as np
        N_NODES = 6250
        N_EDGES = 100000
        N_REL = 8
        DIM = 256

        def _rgcn_layer(x, W, b, src, dst, edge_type, num_nodes):
            xt = jnp.einsum('ni,rio->rno', x, W)
            msg = jax.nn.relu(xt[edge_type, src] + b)
            return jax.ops.segment_sum(msg, dst, num_segments=num_nodes)
        key = jax.random.key(seed)
        ks = jax.random.split(key, 6)
        x = jax.random.normal(ks[0], (N_NODES, DIM), dtype=jnp.float32)
        limit = float(np.sqrt(6.0 / (DIM + DIM)))
        W0 = jax.random.uniform(ks[1], (N_REL, DIM, DIM), dtype=jnp.float32, minval=-limit, maxval=limit)
        W1 = jax.random.uniform(ks[2], (N_REL, DIM, DIM), dtype=jnp.float32, minval=-limit, maxval=limit)
        b0 = jnp.zeros((DIM,), dtype=jnp.float32)
        b1 = jnp.zeros((DIM,), dtype=jnp.float32)
        edge_index = jax.random.randint(ks[3], (2, N_EDGES), 0, N_NODES, dtype=jnp.int64)
        edge_type = jax.random.randint(ks[4], (N_EDGES,), 0, N_REL, dtype=jnp.int64)
        return {'x': x, 'W0': W0, 'b0': b0, 'W1': W1, 'b1': b1, 'edge_index': edge_index, 'edge_type': edge_type}
    _L0_gnn_all = _L0_gnn_setup()
    _L0_gnn_in = {k: v for k, v in _L0_gnn_all.items() if k in ('W0', 'b0', 'W1', 'b1')}
    del _L0_gnn_all

    def _L0_ffn_setup():
        import jax, jax.numpy as jnp
        import numpy as np
        DIM = 256
        H = 8
        D = 64
        G = 64
        INNER = H * D
        SCALE = D ** (-0.5)
        key = jax.random.key(seed)
        ks = jax.random.split(key, 12)
        B, N = (4, 2048)
        x = jax.random.normal(ks[0], (B, N, DIM), dtype=jnp.float32)
        s = lambda fan_in: 1.0 / np.sqrt(fan_in)
        W_fx = jax.random.normal(ks[1], (DIM, INNER), dtype=jnp.float32) * s(DIM)
        b_fx = jnp.zeros((INNER,), dtype=jnp.float32)
        W_x = jax.random.normal(ks[2], (DIM, INNER), dtype=jnp.float32) * s(DIM)
        b_x = jnp.zeros((INNER,), dtype=jnp.float32)
        A = jax.random.normal(ks[3], (G, D), dtype=jnp.float32)
        Q, _ = jnp.linalg.qr(A.T)
        W_slice = Q[:, :G].astype(jnp.float32)
        b_slice = jnp.zeros((G,), dtype=jnp.float32)
        W_q = jax.random.normal(ks[4], (D, D), dtype=jnp.float32) * s(D)
        W_k = jax.random.normal(ks[5], (D, D), dtype=jnp.float32) * s(D)
        W_v = jax.random.normal(ks[6], (D, D), dtype=jnp.float32) * s(D)
        W_out = jax.random.normal(ks[7], (INNER, DIM), dtype=jnp.float32) * s(INNER)
        b_out = jnp.zeros((DIM,), dtype=jnp.float32)
        temperature = jnp.ones((1, H, 1, 1), dtype=jnp.float32) * 0.5
        return {'x': x, 'W_fx': W_fx, 'b_fx': b_fx, 'W_x': W_x, 'b_x': b_x, 'W_slice': W_slice, 'b_slice': b_slice, 'W_q': W_q, 'W_k': W_k, 'W_v': W_v, 'W_out': W_out, 'b_out': b_out, 'temperature': temperature}
    _L0_ffn_all = _L0_ffn_setup()
    _L0_ffn_in = {k: v for k, v in _L0_ffn_all.items() if k in ('W_fx', 'b_fx', 'W_x', 'b_x', 'W_slice', 'b_slice', 'W_q', 'W_k', 'W_v', 'W_out', 'b_out', 'temperature')}
    del _L0_ffn_all
    return {'x': x, 'src': src, 'dst': dst, 'edge_type_8': edge_type_8, 'L0_gnn_W0': _L0_gnn_in['W0'], 'L0_gnn_b0': _L0_gnn_in['b0'], 'L0_gnn_W1': _L0_gnn_in['W1'], 'L0_gnn_b1': _L0_gnn_in['b1'], 'L0_ffn_W_fx': _L0_ffn_in['W_fx'], 'L0_ffn_b_fx': _L0_ffn_in['b_fx'], 'L0_ffn_W_x': _L0_ffn_in['W_x'], 'L0_ffn_b_x': _L0_ffn_in['b_x'], 'L0_ffn_W_slice': _L0_ffn_in['W_slice'], 'L0_ffn_b_slice': _L0_ffn_in['b_slice'], 'L0_ffn_W_q': _L0_ffn_in['W_q'], 'L0_ffn_W_k': _L0_ffn_in['W_k'], 'L0_ffn_W_v': _L0_ffn_in['W_v'], 'L0_ffn_W_out': _L0_ffn_in['W_out'], 'L0_ffn_b_out': _L0_ffn_in['b_out'], 'L0_ffn_temperature': _L0_ffn_in['temperature']}

def reference(x, src, dst, edge_type_8, L0_gnn_W0, L0_gnn_b0, L0_gnn_W1, L0_gnn_b1, L0_ffn_W_fx, L0_ffn_b_fx, L0_ffn_W_x, L0_ffn_b_x, L0_ffn_W_slice, L0_ffn_b_slice, L0_ffn_W_q, L0_ffn_W_k, L0_ffn_W_v, L0_ffn_W_out, L0_ffn_b_out, L0_ffn_temperature):
    import jax
    import jax.numpy as jnp

    def _L0_gnn_ref(x, W0, b0, W1, b1, edge_index, edge_type):
        import jax, jax.numpy as jnp
        import numpy as np
        N_NODES = 6250
        N_EDGES = 100000
        N_REL = 8
        DIM = 256

        def _rgcn_layer(x, W, b, src, dst, edge_type, num_nodes):
            xt = jnp.einsum('ni,rio->rno', x, W)
            msg = jax.nn.relu(xt[edge_type, src] + b)
            return jax.ops.segment_sum(msg, dst, num_segments=num_nodes)
        src, dst = (edge_index[0], edge_index[1])
        h = _rgcn_layer(x, W0, b0, src, dst, edge_type, x.shape[0])
        h = _rgcn_layer(h, W1, b1, src, dst, edge_type, x.shape[0])
        return h

    def _L0_ffn_ref(x, W_fx, b_fx, W_x, b_x, W_slice, b_slice, W_q, W_k, W_v, W_out, b_out, temperature):
        import jax, jax.numpy as jnp
        import numpy as np
        DIM = 256
        H = 8
        D = 64
        G = 64
        INNER = H * D
        SCALE = D ** (-0.5)
        B, N, _ = x.shape
        fx_mid = (x @ W_fx + b_fx).reshape(B, N, H, D).transpose(0, 2, 1, 3)
        x_mid = (x @ W_x + b_x).reshape(B, N, H, D).transpose(0, 2, 1, 3)
        temp = jnp.clip(temperature, 0.1, 5.0)
        slice_weights = jax.nn.softmax((x_mid @ W_slice + b_slice) / temp, axis=-1)
        slice_norm = slice_weights.sum(axis=2)
        slice_token = jnp.einsum('bhnc,bhng->bhgc', fx_mid, slice_weights)
        slice_token = slice_token / (slice_norm[..., None] + 1e-05)
        q = slice_token @ W_q
        k = slice_token @ W_k
        v = slice_token @ W_v
        attn = jax.nn.softmax(jnp.einsum('bhgc,bhkc->bhgk', q, k) * SCALE, axis=-1)
        out_slice = jnp.einsum('bhgk,bhkc->bhgc', attn, v)
        out_x = jnp.einsum('bhgc,bhng->bhnc', out_slice, slice_weights)
        out_x = out_x.transpose(0, 2, 1, 3).reshape(B, N, INNER)
        return out_x @ W_out + b_out
    edge_index = jnp.stack([src, dst])
    x = x + _L0_gnn_ref(_layernorm(x, axis=-1), L0_gnn_W0, L0_gnn_b0, L0_gnn_W1, L0_gnn_b1, edge_index, edge_type_8)
    x = x + _L0_ffn_ref(_layernorm(x, axis=-1)[None], L0_ffn_W_fx, L0_ffn_b_fx, L0_ffn_W_x, L0_ffn_b_x, L0_ffn_W_slice, L0_ffn_b_slice, L0_ffn_W_q, L0_ffn_W_k, L0_ffn_W_v, L0_ffn_W_out, L0_ffn_b_out, L0_ffn_temperature)[0]
    return x

_drawn_inputs = setup_inputs


def setup_inputs(seed=0):
    import zlib

    import numpy as np

    out = dict(_drawn_inputs(seed))
    spreads = {'L0_gnn_b0': (0.0, 0.1),
     'L0_gnn_b1': (0.0, 0.8),
     'L0_ffn_b_fx': (0.0, 0.8),
     'L0_ffn_b_x': (0.0, 0.8),
     'L0_ffn_b_slice': (0.0, 0.8),
     'L0_ffn_b_out': (0.0, 0.8),
     'L0_ffn_temperature': (0.5, 0.6)}
    factors = {'L0_ffn_W_fx': 8.0,
     'L0_ffn_W_x': 8.0,
     'L0_ffn_W_slice': 8.0,
     'L0_ffn_W_q': 8.0,
     'L0_ffn_W_k': 8.0,
     'L0_ffn_W_v': 8.0,
     'L0_ffn_W_out': 8.0}
    for name, (base, spread) in spreads.items():
        noise = np.random.default_rng([zlib.crc32(name.encode()), seed]).standard_normal(out[name].shape)
        drawn = base * np.exp(spread * noise) if base else spread * noise
        out[name] = jnp.asarray(drawn.astype(out[name].dtype))
    for name, factor in factors.items():
        out[name] = (out[name] * factor).astype(out[name].dtype)
    return out
```

```python
from contextlib import ExitStack, contextmanager

import concourse.bass as bass
from concourse import mybir

ALU = mybir.AluOpType
ACT = mybir.ActivationFunctionType
F32 = mybir.dt.float32
I32 = mybir.dt.int32
AX_X = mybir.AxisListType.X

P = 128
OFFSET = 32
STEP = 64
TILES = 16
QUAD = 4
HALVES = 2
LN_EPS = 1e-5
NORM_EPS = 1e-5


class Chain:

    def __init__(self, engine, semaphore):
        self.engine, self.semaphore, self.base, self.steps = engine, semaphore, 0, 0

    def __call__(self, instruction):
        self.steps += 1
        instruction.then_inc(self.semaphore, 1)
        self.engine.wait_ge(self.semaphore, self.base + self.steps)

    @contextmanager
    def loop(self, count, steps):
        base, before = self.base, self.steps
        with self.engine.Fori(0, count) as i:
            self.base, self.steps = base + before + i * steps, 0
            yield i
            assert self.steps == steps, f"{self.steps} steps"
        self.base, self.steps = base, before + count * steps


def build_program(nc, x, src, dst, edge_type, w0, b0, w1, b1, w_fx, b_fx, w_x, b_x, w_slice, b_slice,
                  w_q, w_k, w_v, w_out, b_out, temperature, out):
    nodes, dim = x.shape
    edges = src.shape[0]
    rels = w0.shape[0]
    inner = w_fx.shape[1]
    head = w_q.shape[0]
    heads = inner // head
    pairs = inner // P
    scale = float(head) ** -0.5
    blocks = -(-(nodes + OFFSET) // P)
    group = TILES * P
    iters = -(-edges // (HALVES * group))
    groups = iters * HALVES
    full_groups = edges // group
    rest = (edges - full_groups * group) // TILES
    tail_rows = nodes + OFFSET - (blocks - 1) * P
    row = rels * dim
    bank = 512
    banks = row // bank
    slots = HALVES * TILES
    quads = slots // QUAD
    half_quads = quads // HALVES
    assert dim == 2 * P and rest * TILES + full_groups * group == edges and full_groups == groups - 1
    assert blocks == iters + 1 and pairs == banks == 4 and head * 2 == P and blocks % 2 == 0

    ctx = ExitStack()
    with ctx:
        def sb(name, shape, dt=F32):
            return ctx.enter_context(nc.sbuf_tensor(name, shape, dt))

        def ps(name):
            return ctx.enter_context(nc.psum_tensor(name, [P, bank], F32))

        def sem(name):
            return ctx.enter_context(nc.semaphore(name))

        table1 = nc.dram_tensor("table1", [blocks * P * rels + rels, dim], F32).ap()
        table2 = nc.dram_tensor("table2", [blocks * P * rels + rels, dim], F32).ap()
        weights_dram = nc.dram_tensor("slice_weights_t", [blocks, P, inner], F32).ap()

        res = sb("res", [P, blocks, dim])
        edge_row = sb("edge_row", [P, (iters + 1) * slots], I32)
        edge_col = sb("edge_col", [P, (iters + 1) * slots])
        edge_dst = sb("edge_dst", [P, (iters + 1) * slots])
        rows_now = sb("rows_now", [P, HALVES, TILES], I32)
        messages = sb("messages", [P, slots, dim])
        onehot = sb("onehot", [P, HALVES, TILES, P])
        w_rel = sb("w_rel", [P, 2, row])
        bias0 = sb("bias0", [P, dim])
        bias1 = sb("bias1", [P, dim])
        table_out = sb("table_out", [P, 2, row])
        ident = sb("ident", [P, P])
        iota_i = sb("iota_i", [P, P], I32)
        iota = sb("iota", [P, P])
        group_base = sb("group_base", [P, groups], I32)
        valid = sb("valid", [P, blocks])
        h_block = sb("h_block", [P, dim])
        carry = sb("carry", [P, dim])
        x_t = sb("x_t", [P, 2, dim])
        xn = sb("xn", [P, dim])
        stats = sb("stats", [P, 6])
        moments = sb("moments", [P, 2])
        std = sb("std", [P, 1])
        rstd = sb("rstd", [P, 1])
        newton = sb("newton", [P, 1])
        spread = sb("spread", [P, 2])
        spread_row = sb("spread_row", [2, P])
        worst = sb("worst", [2, 1])
        worst_row = sb("worst_row", [1, 1])
        flag = sb("flag", [1, 1], I32)
        dst_now = sb("dst_now", [P, TILES])
        zero_tile = sb("zero_tile", [P, dim + 1])
        x2 = sb("x2", [P, dim])
        xn2 = sb("xn2", [P, dim + 1])
        bias_out = sb("bias_out", [P, dim])
        w_fold = sb("w_fold", [P, 2, inner])
        bias_fold = sb("bias_fold", [P, inner])
        temp = sb("temp", [P, heads])
        b_slice_all = sb("b_slice_all", [P, head])
        logits = sb("logits", [P, inner])
        slice_w = sb("slice_w", [P, inner])
        head_max = sb("head_max", [P, heads])
        head_sum = sb("head_sum", [P, heads])
        weights_t = sb("weights_t", [P, inner])
        w_fx_sb = sb("w_fx_sb", [P, 2, inner])
        b_fx_row = sb("b_fx_row", [1, inner])
        w_out_sb = sb("w_out_sb", [P, pairs, dim])
        diag_w = sb("diag_w", [P, 4, P])
        typ_i = messages[:, 0:13, :].rearrange("p a b -> p (a b)").bitcast(I32)
        dst_i = messages[:, 13:26, :].rearrange("p a b -> p (a b)").bitcast(I32)
        b_x_rows = logits[0:pairs, 0:P]
        b_x_t = slice_w[:, 0:pairs]
        w_x_sb = table_out[:, 0, 0:2 * inner].rearrange("p (k n) -> p k n", k=2)
        w_x_t = table_out[:, 0, 2 * inner:4 * inner].rearrange("p (k n) -> p k n", k=2)
        b_x_wide = table_out[:, 1, 0:inner]
        zeros_row = onehot[0:1, :, :, :].rearrange("p a t c -> p (a t c)")[:, 0:row]
        mes = messages[:, :, :].rearrange("p t d -> p (t d)")
        tokens = mes[:, 0:pairs * (dim + 1)].rearrange("p (q n) -> p q n", q=pairs)

        def stage4(n):
            return mes[:, 1100 + n * inner:1100 + (n + 1) * inner]

        tok_t0, tok_t1, tok_diag, q_t, k_t, v_sb, attn, attn_diag, attn_t, os_t = (stage4(n) for n in range(10))
        norm_row = mes[0:1, 6300:6300 + inner]
        tok_rn = mes[:, 6900:6900 + pairs]
        attn_max = mes[:, 6904:6904 + pairs]
        attn_sum = mes[:, 6908:6908 + pairs]
        mix = table_out[:, 0, 0:pairs * dim].rearrange("p (q n) -> p q n", q=pairs)
        out_slots = 4
        w_in = w_rel[:, :, :].rearrange("p k n -> p (k n)")[:, 0:out_slots * inner].rearrange(
            "p (s n) -> p s n", s=out_slots)
        y_out = table_out[:, 1, 0:out_slots * dim].rearrange("p (s n) -> p s n", s=out_slots)

        ps_sum = [ps("ps_sum0"), ps("ps_sum1")]
        ps_tr = ps("ps_tr")
        ps_x = ps("ps_x")
        ps_q = [ps(f"ps_q{c}") for c in range(banks)]

        s_zero_rows = sem("s_zero_rows")
        s_x = [sem("s_x0"), sem("s_x1")]
        s_edges = sem("s_edges")
        s_small = sem("s_small")
        s_late = sem("s_late")
        s_w0 = sem("s_w0")
        s_w1 = sem("s_w1")
        s_wslot = [sem(f"s_wslot{s}") for s in range(out_slots)]
        s_pool_const = sem("s_pool_const")
        s_pads = sem("s_pads")
        s_const = sem("s_const")
        s_zeros = sem("s_zeros")
        s_diag_zero = sem("s_diag_zero")
        s_zero_row_stored = sem("s_zero_row_stored")
        s_fold_pe = sem("s_fold_pe")
        s_fold_dve = sem("s_fold_dve")
        s_spread = sem("s_spread")
        s_spread_pe = sem("s_spread_pe")
        s_flag = sem("s_flag")
        s_var = sem("s_var")
        s_std = sem("s_std")
        s_xn = sem("s_xn")
        s_tr = sem("s_tr")
        s_tr_copied = sem("s_tr_copied")
        s_tab_mm = [sem(f"s_tab_mm{c}") for c in range(banks)]
        s_tab_sum = [sem(f"s_tab_sum{c}") for c in range(banks)]
        s_relu = sem("s_relu")
        s_stored = [sem("s_stored0"), sem("s_stored1")]
        s_rows = [sem("s_rows0"), sem("s_rows1")]
        s_onehot = [sem("s_onehot0"), sem("s_onehot1")]
        s_gathered = [sem(f"s_gathered{q}") for q in range(quads)]
        s_used = [sem(f"s_used{q}") for q in range(quads)]
        s_sum_free = [sem("s_sum_free0"), sem("s_sum_free1")]
        s_h = sem("s_h")
        s_g_rows = sem("s_g_rows")
        s_g_gathered = [sem(f"s_g_gathered{q}") for q in range(half_quads)]
        s_g_onehot = sem("s_g_onehot")
        s_g_mm = sem("s_g_mm")
        s_g_added = sem("s_g_added")
        s_g_clear = sem("s_g_clear")
        s_g_x = sem("s_g_x")
        s_logits = sem("s_logits")
        s_shifted = sem("s_shifted")
        s_exp = sem("s_exp")
        s_slice_w = sem("s_slice_w")
        s_tokens = sem("s_tokens")
        s_w_tr = sem("s_w_tr")
        s_w_copied = sem("s_w_copied")
        s_w_stored = sem("s_w_stored")
        s_w_free = sem("s_w_free")
        s_c_pe = sem("s_c_pe")
        s_c_dve = sem("s_c_dve")
        s_c_exp = sem("s_c_exp")
        s_o_mm = sem("s_o_mm")
        s_o_sum = sem("s_o_sum")
        s_o_stored = [sem(f"s_o_stored{s}") for s in range(out_slots)]
        s_held_dve = sem("s_held_dve")
        s_held_pool = sem("s_held_pool")
        s_held_pe = sem("s_held_pe")
        s_dve_a = sem("s_dve_a")
        s_dve_f = sem("s_dve_f")
        s_dve_g = sem("s_dve_g")
        s_dve_c = sem("s_dve_c")

        (C_TOKENS, C_TT, C_DIAG, C_QKV, C_SHIFTED, C_ATTN, C_ATTN_T, C_OS, C_MIX) = range(1, 10)
        (E_TT, E_TOK, E_QKV, E_LOGITS, E_ATTN_T, E_OS, E_MIX) = range(1, 8)

        def hold(engine, semaphore):
            engine.sem_inc(semaphore, 1)

        def at(tile, k, width):
            if isinstance(k, int):
                return tile[:, k * width:(k + 1) * width]
            return tile[:, bass.ds(k * width, width)]

        res_flat = res[:, :, :].rearrange("p k d -> p (k d)")

        def res_at(k):
            return at(res_flat, k, dim)

        def table_rows(table, k):
            view = table[0:blocks * P * rels, :].rearrange("(k p r) o -> k p (r o)", p=P, r=rels)
            return view[k] if isinstance(k, int) else view[bass.ds(k, 1)].rearrange("a p n -> (a p) n")

        block = ctx.enter_context(nc.Block())

        @block.sync
        def _(sp):
            sp.sem_inc(s_w_free, 1)

            def load_x_edges(semaphore):
                sp.dma_start(res[OFFSET:P, 0, :], x[0:P - OFFSET, :]).then_inc(semaphore, 16)
                sp.dma_start(res[0:tail_rows, blocks - 1, :], x[nodes - tail_rows:nodes, :]).then_inc(semaphore, 16)

            def load_x(first, last, semaphore):
                view = x[P - OFFSET:nodes - tail_rows, :].rearrange("(k p) d -> p k d", p=P)
                sp.dma_start(res[:, first:last, :], view[:, first - 1:last - 1, :]).then_inc(semaphore, 16)

            def load_w(w, semaphore):
                for k in range(2):
                    sp.dma_start(w_rel[:, k, :].rearrange("p (r o) -> p r o", r=rels),
                                 w[:, k * P:(k + 1) * P, :].rearrange("r p o -> p r o")).then_inc(semaphore, 16)

            def store_table(n, k, slot, table):
                sp.wait_ge(s_relu, (n + 1) * banks)
                sp.dma_start(table_rows(table, k), table_out[:, slot, :]).then_inc(s_stored[slot], 16)

            def store_weights(k):
                sp.wait_ge(s_w_copied, k + 2)
                view = weights_dram[k] if isinstance(k, int) else \
                    weights_dram[bass.ds(k, 1)].rearrange("a p n -> (a p) n")
                sp.dma_start(view, weights_t[:, :]).then_inc(s_w_stored, 16)
                sp.wait_ge(s_w_stored, (k + 1) * 16)
                sp.sem_inc(s_w_free, 1)

            sp.dma_start(w_x_sb, w_x.rearrange("(k p) n -> p k n", p=P)).then_inc(s_small, 16)
            sp.dma_start(b_x_rows, b_x.rearrange("(q p) -> q p", p=P)).then_inc(s_small, 16)
            sp.dma_start(temp[:, :], temperature.rearrange("a h b c -> (a b c) h").to_broadcast([P, heads])
                         ).then_inc(s_small, 16)
            sp.dma_start(b_slice_all[:, :], b_slice.unsqueeze(0).to_broadcast([P, head])).then_inc(s_small, 16)
            sp.dma_start(bias0[:, :], b0.unsqueeze(0).to_broadcast([P, dim])).then_inc(s_small, 16)
            sp.dma_start(bias1[:, :], b1.unsqueeze(0).to_broadcast([P, dim])).then_inc(s_small, 16)
            sp.dma_start(bias_out[:, :], b_out.unsqueeze(0).to_broadcast([P, dim])).then_inc(s_small, 16)
            sp.wait_ge(s_diag_zero, 1)
            for n, w in enumerate((w_slice, w_q, w_k, w_v)):
                for a in range(2):
                    sp.dma_start(diag_w[a * head:(a + 1) * head, n, a * head:(a + 1) * head], w
                                 ).then_inc(s_small, 16)
            sp.wait_ge(s_zero_rows, 1)
            load_x_edges(s_x[0])
            load_x(1, 5, s_x[0])
            load_w(w0, s_w0)
            load_x(5, blocks - 1, s_x[1])
            sp.dma_start(w_fx_sb[:, :, :], w_fx.rearrange("(k p) n -> p k n", p=P)).then_inc(s_late, 16)
            sp.dma_start(b_fx_row[:, :], b_fx.unsqueeze(0)).then_inc(s_late, 16)
            sp.dma_start(w_out_sb[:, :, :], w_out.rearrange("(q p) n -> p q n", p=P)).then_inc(s_late, 16)
            sp.wait_ge(s_pads, 1)
            for i, (tile, values) in enumerate(((edge_row, src), (typ_i, edge_type), (dst_i, dst))):
                view = tile[:, 0:groups * TILES].rearrange("p (g t) -> p g t", t=TILES)
                sp.dma_start(view[:, 0:full_groups, :],
                             values[0:full_groups * group].rearrange("(g p t) -> p g t", p=P, t=TILES)
                             ).then_inc(s_edges, 16)
                sp.dma_start(view[0:rest, full_groups, :],
                             values[full_groups * group:edges].rearrange("(p t) -> p t", t=TILES)
                             ).then_inc(s_edges, 16)
            sp.wait_ge(s_zeros, 1)
            for table in (table1, table2):
                sp.dma_start(table[blocks * P * rels:, :].rearrange("(a r) o -> a (r o)", a=1),
                             zeros_row).then_inc(s_zero_row_stored, 16)
            with sp.Fori(0, blocks // 2) as i:
                for s in range(2):
                    store_table(i * 2 + s, i * 2 + s, s, table1)
            sp.wait_ge(s_tab_mm[banks - 1], blocks)
            load_w(w1, s_w1)
            sp.wait_ge(s_flag, 1)
            general = sp.value_load(flag[0:1, 0:1], min_val=0, max_val=1)
            with sp.If(general == 0):
                with sp.Fori(0, iters) as k:
                    store_table(k + blocks, k, 0, table2)
                store_table(2 * blocks - 1, blocks - 1, 0, table2)
                with sp.Fori(0, iters) as k:
                    store_weights(k)
                store_weights(blocks - 1)
            with sp.Else():
                with sp.Fori(0, blocks) as k:
                    store_table(k + blocks, k, 0, table2)
                sp.wait_ge(s_g_clear, 1)
                load_x_edges(s_g_x)
                load_x(1, blocks - 1, s_g_x)
                with sp.Fori(0, blocks) as k:
                    store_weights(k)
            sp.nop()

            def load_weights(k, slot):
                if not isinstance(k, int) or k >= out_slots:
                    sp.wait_ge(s_o_mm, k - (out_slots - 1))
                view = weights_dram[k] if isinstance(k, int) else \
                    weights_dram[bass.ds(k, 1)].rearrange("a p n -> (a p) n")
                sp.dma_start(w_in[:, slot, :], view).then_inc(s_wslot[slot], 16)

            for k in range(out_slots):
                load_weights(k, k)
            with sp.Fori(0, (blocks - 2) // out_slots - 1) as i:
                for s in range(out_slots):
                    load_weights(i * out_slots + (out_slots + s), s)
            for k in range(blocks - 2, blocks):
                load_weights(k, k % out_slots)

        @block.gpsimd
        def _(pool):
            pool.memset(ident[:, :], 0.0).then_inc(s_pool_const, 1)
            pool.memset(valid[:, :], 1.0).then_inc(s_pool_const, 1)
            pool.wait_ge(s_pool_const, 2)
            pool.affine_select(out=ident[:, :], in_=ident[:, :], compare_op=ALU.not_equal, fill=1.0,
                               base=0, pattern=[[-1, P]], channel_multiplier=1).then_inc(s_pool_const, 1)
            pool.affine_select(out=valid[:, 0:1], in_=valid[:, 0:1], compare_op=ALU.is_ge, fill=0.0,
                               base=-OFFSET, pattern=[[0, 1]], channel_multiplier=1).then_inc(s_pool_const, 1)
            pool.affine_select(out=valid[:, blocks - 1:blocks], in_=valid[:, blocks - 1:blocks],
                               compare_op=ALU.is_ge, fill=0.0, base=tail_rows - 1, pattern=[[0, 1]],
                               channel_multiplier=-1).then_inc(s_pool_const, 1)
            pool.iota(iota_i[:, :], pattern=[[1, P]], base=0, channel_multiplier=0).then_inc(s_pool_const, 1)
            pool.iota(group_base[:, :], pattern=[[STEP, groups]], base=0, channel_multiplier=0
                      ).then_inc(s_pool_const, 1)

            def gather(table, slot, half, t, semaphore):
                pool.indirect_dma_start(
                    out=messages[:, slot, :], out_offset=None, in_=table,
                    in_offset=bass.IndirectOffsetOnAxis(ap=rows_now[:, half, t:t + 1], axis=0)
                ).then_inc(semaphore, 16)

            def gather_iteration(table, i):
                for h in range(HALVES):
                    pool.wait_ge(s_rows[h], i + 1)
                    for j in range(half_quads):
                        q = h * half_quads + j
                        pool.wait_ge(s_used[q], i + 1)
                        hold(pool, s_held_pool)
                        for t in range(QUAD):
                            gather(table, q * QUAD + t, h, j * QUAD + t, s_gathered[q])

            pool.wait_ge(s_flag, 1)
            general = pool.value_load(flag[0:1, 0:1], min_val=0, max_val=1)
            pool.wait_ge(s_zero_row_stored, 32)
            for s in range(2):
                pool.wait_ge(s_stored[s], 16 * (blocks // 2))
            with pool.If(general == 0):
                with pool.Fori(0, iters) as i:
                    gather_iteration(table1, i)
                pool.wait_ge(s_stored[0], 16 * (blocks // 2 + blocks))
                with pool.Fori(0, iters) as i:
                    gather_iteration(table2, i + iters)
            with pool.Else():
                for layer, table in enumerate((table1, table2)):
                    if layer:
                        pool.wait_ge(s_stored[0], 16 * (blocks // 2 + blocks))
                    with pool.Fori(0, groups) as g:
                        pool.wait_ge(s_g_rows, g + (layer * groups + 1))
                        pool.wait_ge(s_g_mm, (g + layer * groups) * blocks + 1)
                        hold(pool, s_held_pool)
                        for t in range(TILES):
                            gather(table, t, 0, t, s_g_gathered[t // QUAD])
            pool.nop()

        @block.scalar
        def _(act):
            act.sem_inc(s_w_copied, 1)

            def root(m):
                act.wait_ge(s_var, m + 1)
                nc.scalar.activation(std[:, :], moments[:, 1:2], ACT.Sqrt).then_inc(s_std, 1)

            def copy_transposed(m, slot):
                act.wait_ge(s_tr, m + 1)
                nc.scalar.activation(x_t[:, slot, :], ps_tr[:, 0:dim], ACT.Copy).then_inc(s_tr_copied, 1)

            def relu(n, c, slot):
                act.wait_ge(s_tab_sum[c], n + 1)
                part = table_out[:, slot, c * bank:(c + 1) * bank]
                nc.scalar.activation(part, part, ACT.Relu).then_inc(s_relu, 1)

            def table_block(k):
                act.wait_ge(s_tab_mm[banks - 1], k + blocks)
                copy_transposed(k + blocks, 0)
                for c in range(banks):
                    relu(k + blocks, c, 0)

            def ffn_block(k):
                root(k + blocks)
                if isinstance(k, int) and k == 0:
                    act.wait_ge(s_tab_mm[banks - 1], 2 * blocks)
                act.wait_ge(s_logits, k + 1)
                copy_transposed(k + 2 * blocks, 0)
                act.wait_ge(s_shifted, k + 1)
                nc.scalar.activation(logits[:, :], logits[:, :], ACT.Exp).then_inc(s_exp, 1)
                act.wait_ge(s_w_tr, k + 2)
                act.wait_ge(s_w_free, k + 1)
                nc.scalar.activation(weights_t[:, :], ps_x[:, :], ACT.Copy).then_inc(s_w_copied, 1)

            root(0)
            copy_transposed(0, 0)

            def table1_block(n, s, last=False):
                if not last:
                    root(n + 1)
                relu(n, 0, s)
                if not last:
                    if not isinstance(n, int) or n:
                        act.wait_ge(s_tab_mm[banks - 1], n)
                    copy_transposed(n + 1, 1 - s)
                for c in range(1, banks):
                    relu(n, c, s)

            for n in range(2):
                table1_block(n, n)
            with act.Fori(1, blocks // 2 - 1) as i:
                for s in range(2):
                    table1_block(i * 2 + s, s)
            table1_block(blocks - 2, 0)
            table1_block(blocks - 1, 1, last=True)

            act.wait_ge(s_flag, 1)
            general = act.value_load(flag[0:1, 0:1], min_val=0, max_val=1)
            with act.If(general == 0):
                with act.Fori(0, iters) as k:
                    table_block(k)
                table_block(blocks - 1)
                act.wait_ge(s_tab_mm[banks - 1], 2 * blocks)
                with act.Fori(0, iters) as k:
                    ffn_block(k)
                ffn_block(blocks - 1)
            with act.Else():
                with act.Fori(0, blocks) as k:
                    table_block(k)
                act.wait_ge(s_tab_mm[banks - 1], 2 * blocks)
                with act.Fori(0, blocks) as k:
                    ffn_block(k)
            act.nop()

            act.wait_ge(s_c_dve, C_SHIFTED)
            nc.scalar.activation(attn[:, 0:pairs * head], attn[:, 0:pairs * head], ACT.Exp).then_inc(s_c_exp, 1)

            def store_out(k, slot, semaphore):
                act.wait_ge(s_o_sum, k + 1)
                if isinstance(k, int) and k == 0:
                    act.dma_start(out[0:P - OFFSET, :], y_out[OFFSET:P, slot, :]).then_inc(semaphore, 16)
                elif isinstance(k, int) and k == blocks - 1:
                    act.dma_start(out[nodes - tail_rows:nodes, :], y_out[0:tail_rows, slot, :]
                                  ).then_inc(semaphore, 16)
                else:
                    view = out[P - OFFSET:nodes - tail_rows, :].rearrange("(k p) d -> k p d", p=P)
                    view = view[k - 1] if isinstance(k, int) else \
                        view[bass.ds(k - 1, 1)].rearrange("a p d -> (a p) d")
                    act.dma_start(view, y_out[:, slot, :]).then_inc(semaphore, 16)

            for k in range(out_slots):
                store_out(k, k, s_o_stored[k])
            with act.Fori(0, (blocks - 2) // out_slots - 1) as i:
                for s in range(out_slots):
                    store_out(i * out_slots + (out_slots + s), s, s_o_stored[s])
            for k in range(blocks - 2, blocks):
                store_out(k, k % out_slots, s_o_stored[k % out_slots])
            for s in range(out_slots):
                act.wait_ge(s_o_stored[s], 16 * len(range(s, blocks, out_slots)))

        @block.vector
        def _(dve):
            vec = nc.vector
            step = Chain(dve, s_dve_a)
            for semaphore in (*s_sum_free, s_g_added):
                dve.sem_inc(semaphore, 1)

            def layer_norm(source, target, m, free):
                step(vec.bn_stats(stats[:, :], source))
                hold(dve, s_held_dve)
                step(vec.bn_aggr(moments[:, :], stats[:, :]))
                vec.tensor_scalar(moments[:, 1:2], moments[:, 1:2], LN_EPS, None, ALU.add).then_inc(s_var, 1)
                dve.wait_ge(s_std, m + 1)
                step(vec.reciprocal(rstd[:, :], std[:, :]))
                step(vec.scalar_tensor_tensor(newton[:, :], rstd[:, :], moments[:, 1:2], rstd[:, :],
                                              ALU.mult, ALU.mult))
                step(vec.tensor_scalar(newton[:, :], newton[:, :], -0.5, 1.5, ALU.mult, ALU.add))
                step(vec.tensor_tensor(rstd[:, :], rstd[:, :], newton[:, :], ALU.mult))
                free()
                vec.tensor_scalar(target, source, moments[:, 0:1], rstd[:, :], ALU.subtract, ALU.mult
                                  ).then_inc(s_xn, 1)

            LN_STEPS = 6

            def add_bias(n, slot, bias, stores):
                if not isinstance(stores, int) or stores:
                    dve.wait_ge(s_stored[slot], stores * 16)
                for c in range(banks):
                    dve.wait_ge(s_tab_mm[c], n + 1)
                    vec.tensor_tensor(
                        table_out[:, slot, c * bank:(c + 1) * bank].rearrange("p (r o) -> p r o", o=dim),
                        ps_q[c][:, :].rearrange("p (r o) -> p r o", o=dim),
                        bias[:, :].unsqueeze(1).to_broadcast([P, bank // dim, dim]), ALU.add
                    ).then_inc(s_tab_sum[c], 1)

            vec.memset(res[:, 0, :], 0.0)
            vec.memset(res[:, blocks - 1, :], 0.0).then_inc(s_zero_rows, 1)
            vec.memset(diag_w[:, :, :], 0.0).then_inc(s_diag_zero, 1)
            pads = slice(full_groups * TILES, groups * TILES)
            vec.memset(edge_row[:, pads], blocks * P - OFFSET)
            vec.memset(typ_i[:, pads], 0)
            vec.memset(dst_i[:, pads], STEP * full_groups).then_inc(s_pads, 1)
            vec.memset(onehot[:, :, :, :], 0.0).then_inc(s_zeros, 1)
            vec.memset(zero_tile[:, :], 0.0).then_inc(s_zeros, 1)
            vec.memset(carry[:, :], 0.0)

            dve.wait_ge(s_small, 16 * 15)
            step(vec.tensor_scalar(temp[:, :], temp[:, :], 0.1, 5.0, ALU.max, ALU.min))
            step(vec.reciprocal(temp[:, :], temp[:, :]))
            dve.wait_ge(s_fold_pe, 1)
            vec.tensor_copy(w_x_t[:, 0, :], ps_sum[0][:, :])
            vec.tensor_copy(w_x_t[:, 1, :], ps_sum[1][:, :])
            step(vec.tensor_copy(b_x_t, ps_tr[:, 0:pairs]))
            vec.tensor_copy(b_x_wide.rearrange("p (q n) -> p q n", q=pairs),
                            b_x_t.unsqueeze(2).to_broadcast([P, pairs, P])).then_inc(s_fold_dve, 1)
            dve.wait_ge(s_fold_pe, 2)
            inv_temp = temp[:, :].unsqueeze(2).to_broadcast([P, heads, head])
            for k, source in enumerate((ps_q[0], ps_q[1])):
                vec.tensor_tensor(w_fold[:, k, :].rearrange("p (h g) -> p h g", h=heads),
                                  source[:, :].rearrange("p (h g) -> p h g", h=heads), inv_temp, ALU.mult)
            fold_heads = bias_fold[:, :].rearrange("p (h g) -> p h g", h=heads)
            step(vec.tensor_tensor(fold_heads, ps_q[2][:, :].rearrange("p (h g) -> p h g", h=heads),
                                   b_slice_all[:, :].unsqueeze(1).to_broadcast([P, heads, head]), ALU.add))
            vec.tensor_tensor(fold_heads, fold_heads, inv_temp, ALU.mult).then_inc(s_fold_dve, 1)

            dve.wait_ge(s_pool_const, 7)
            step(vec.tensor_copy(iota[:, :], iota_i[:, :]))
            dve.wait_ge(s_x[0], 48)
            layer_norm(res_at(0), xn[:, :], 0, lambda: None)

            def table1_block(n, slot, stores, last=False):
                if not last:
                    layer_norm(res_at(n + 1), xn[:, :], n + 1,
                               lambda: dve.wait_ge(s_tr, n + 1))
                add_bias(n, slot, bias0, stores)

            for n in range(4):
                table1_block(n, n % 2, n // 2)
            dve.wait_ge(s_x[1], 16)
            with step.loop(blocks // 2 - 3, 2 * LN_STEPS) as i:
                for s in range(2):
                    table1_block(i * 2 + (4 + s), s, i + 2)
            table1_block(blocks - 2, 0, blocks // 2 - 1)
            table1_block(blocks - 1, 1, blocks // 2 - 1, last=True)

            real = slice(0, groups * TILES)
            dve.wait_ge(s_edges, 16 * 6)
            step(vec.scalar_tensor_tensor(edge_row[:, real], edge_row[:, real], float(rels), typ_i[:, real],
                                          ALU.mult, ALU.add))
            step(vec.tensor_scalar(edge_row[:, real], edge_row[:, real], float(OFFSET * rels), None, ALU.add))
            step(vec.tensor_scalar(dst_i[:, real], dst_i[:, real], float(OFFSET), None, ALU.add))
            step(vec.tensor_copy(edge_dst[:, real], dst_i[:, real]))
            step(vec.tensor_tensor(edge_col[:, real].rearrange("p (g t) -> p g t", t=TILES),
                                   edge_dst[:, real].rearrange("p (g t) -> p g t", t=TILES),
                                   group_base[:, :].unsqueeze(2).to_broadcast([P, groups, TILES]), ALU.subtract))
            vec.tensor_reduce(spread[:, 0:1], edge_col[:, real], AX_X, ALU.max)
            step(vec.tensor_reduce(spread[:, 1:2], edge_col[:, real], AX_X, ALU.min))
            vec.tensor_scalar(spread[:, 0:1], spread[:, 0:1], float(1 - P), None, ALU.add)
            vec.tensor_scalar(spread[:, 1:2], spread[:, 1:2], -1.0, None, ALU.mult).then_inc(s_spread, 1)
            step(vec.tensor_scalar(dst_i[:, real], dst_i[:, real], P - 1, None, ALU.bitwise_and))
            step(vec.tensor_copy(edge_col[:, real], dst_i[:, real]))
            wrap = slice(iters * slots, (iters + 1) * slots)
            vec.tensor_copy(edge_row[:, wrap], edge_row[:, 0:slots])
            step(vec.tensor_copy(edge_col[:, wrap], edge_col[:, 0:slots]))
            dve.wait_ge(s_spread_pe, 1)
            step(vec.tensor_reduce(worst[:, :], ps_tr[0:2, 0:P], AX_X, ALU.max))
            dve.sem_inc(s_spread, 1)
            dve.wait_ge(s_spread_pe, 2)
            step(vec.tensor_reduce(worst_row[:, :], ps_tr[0:1, 0:2], AX_X, ALU.max))
            vec.tensor_scalar(flag[:, :], worst_row[:, :], 0.0, None, ALU.is_gt).then_inc(s_flag, 1)

            def prepare(h, i, k):
                at_half = at(edge_col, k * HALVES + h, TILES)
                vec.tensor_copy(rows_now[:, h, :], at(edge_row, k * HALVES + h, TILES)).then_inc(s_rows[h], 1)
                vec.tensor_tensor(onehot[:, h, :, :], iota[:, :].unsqueeze(1).to_broadcast([P, TILES, P]),
                                  at_half.unsqueeze(2).to_broadcast([P, TILES, P]), ALU.is_equal
                                  ).then_inc(s_onehot[h], 1)

            dve.wait_ge(s_zero_row_stored, 32)
            for h in range(HALVES):
                prepare(h, 0, 0)

            def softmax_block(k):
                step(vec.tensor_tensor(res_at(k), x2[:, :], bias_out[:, :], ALU.add))
                step(vec.tensor_copy(xn2[:, dim:dim + 1], at(valid, k, 1)))
                layer_norm(x2[:, :], xn2[:, 0:dim], k + blocks, lambda: None)
                dve.wait_ge(s_logits, k + 2)
                step(vec.tensor_tensor(logits[:, :], ps_x[:, :], bias_fold[:, :], ALU.add))
                by_head = logits[:, :].rearrange("p (h g) -> p h g", h=heads)
                step(vec.tensor_reduce(head_max[:, :], by_head, AX_X, ALU.max))
                vec.tensor_tensor(by_head, by_head, head_max[:, :].unsqueeze(2).to_broadcast([P, heads, head]),
                                  ALU.subtract).then_inc(s_shifted, 1)
                dve.wait_ge(s_exp, k + 1)
                step(vec.tensor_reduce(head_sum[:, :], by_head, AX_X, ALU.add))
                step(vec.reciprocal(head_sum[:, :], head_sum[:, :]))
                vec.tensor_tensor(slice_w[:, :].rearrange("p (h g) -> p h g", h=heads), by_head,
                                  head_sum[:, :].unsqueeze(2).to_broadcast([P, heads, head]), ALU.mult
                                  ).then_inc(s_slice_w, 1)

            SOFTMAX_STEPS = 6 + LN_STEPS
            dve.wait_ge(s_flag, 1)
            general = dve.value_load(flag[0:1, 0:1], min_val=0, max_val=1)
            with dve.If(general == 0):
                step = Chain(dve, s_dve_f)

                def combine(i, k):
                    last = half_quads - 1
                    dve.wait_ge(s_used[last], i + 2)
                    step(vec.tensor_tensor(h_block[:, :], ps_sum[0][:, 0:dim], carry[:, :], ALU.add))
                    dve.sem_inc(s_sum_free[0], 1)
                    prepare(0, i + 1, k + 1)
                    dve.wait_ge(s_used[quads - 1], i + 2)
                    step(vec.tensor_tensor(h_block[STEP:P, :], h_block[STEP:P, :], ps_sum[1][STEP:P, 0:dim],
                                           ALU.add))
                    step(vec.tensor_copy(carry[0:STEP, :], ps_sum[1][0:STEP, 0:dim]))
                    dve.sem_inc(s_sum_free[1], 1)
                    prepare(1, i + 1, k + 1)

                COMBINE_STEPS = 3

                with step.loop(iters, COMBINE_STEPS) as k:
                    dve.wait_ge(s_tr, k + blocks)
                    combine(k, k)
                    dve.sem_inc(s_h, 1)
                    add_bias(k + blocks, 0, bias1, k + blocks // 2)
                dve.wait_ge(s_tr, 2 * blocks - 1)
                step(vec.tensor_copy(h_block[:, :], carry[:, :]))
                dve.sem_inc(s_h, 1)
                step(vec.memset(carry[:, :], 0.0))
                add_bias(2 * blocks - 1, 0, bias1, blocks // 2 + blocks - 1)
                dve.wait_ge(s_tr, 2 * blocks)
                with step.loop(iters, COMBINE_STEPS + 1 + SOFTMAX_STEPS) as k:
                    combine(k + iters, k)
                    dve.wait_ge(s_tokens, k + 1)
                    dve.wait_ge(s_w_tr, k + 1)
                    step(vec.tensor_tensor(x2[:, :], res_at(k), h_block[:, :], ALU.add))
                    softmax_block(k)
                dve.wait_ge(s_tokens, blocks)
                dve.wait_ge(s_w_tr, blocks)
                step(vec.tensor_tensor(x2[:, :], res_at(blocks - 1), carry[:, :], ALU.add))
                softmax_block(blocks - 1)
            with dve.Else():
                step = Chain(dve, s_dve_g)
                for layer in range(2):
                    if layer == 0:
                        dve.wait_ge(s_tr, blocks)
                        step(vec.memset(res[:, :, :], 0.0))
                    else:
                        step(vec.memset(res[:, 0, :], 0.0))
                        step(vec.memset(res[:, blocks - 1, :], 0.0))
                        dve.sem_inc(s_g_clear, 1)
                        dve.wait_ge(s_g_x, 48)
                    with step.loop(groups, 1 + 3 * blocks) as g:
                        done = (g + layer * groups) * blocks
                        dve.wait_ge(s_g_mm, done + 1)
                        vec.tensor_copy(rows_now[:, 0, :], at(edge_row, g, TILES)).then_inc(s_g_rows, 1)
                        step(vec.tensor_copy(dst_now[:, :], at(edge_dst, g, TILES)))
                        hold(dve, s_held_dve)
                        with step.loop(blocks, 3) as w:
                            step(vec.tensor_tensor(
                                onehot[:, 0, :, :], iota[:, :].unsqueeze(1).to_broadcast([P, TILES, P]),
                                dst_now[:, :].unsqueeze(2).to_broadcast([P, TILES, P]), ALU.is_equal))
                            dve.sem_inc(s_g_onehot, 1)
                            step(vec.tensor_scalar(dst_now[:, :], dst_now[:, :], float(P), None, ALU.subtract))
                            dve.wait_ge(s_g_mm, done + w + 2)
                            step(vec.tensor_tensor(res_at(w), res_at(w), ps_sum[0][:, 0:dim], ALU.add))
                            dve.sem_inc(s_g_added, 1)
                    if layer == 0:
                        with step.loop(blocks, 1) as k:
                            dve.wait_ge(s_tr, k + blocks)
                            step(vec.tensor_copy(h_block[:, :], res_at(k)))
                            dve.sem_inc(s_h, 1)
                            add_bias(k + blocks, 0, bias1, k + blocks // 2)
                    else:
                        with step.loop(blocks, 1 + SOFTMAX_STEPS) as k:
                            dve.wait_ge(s_tokens, k + 1)
                            dve.wait_ge(s_w_tr, k + 1)
                            step(vec.tensor_copy(x2[:, :], res_at(k)))
                            softmax_block(k)
            dve.nop()

            step = Chain(dve, s_dve_c)

            def done():
                dve.sem_inc(s_c_dve, 1)

            def two(tile, a, width):
                return tile.rearrange("p (q n) -> p q n", q=pairs)[a * head:(a + 1) * head, :,
                                                                   a * width:a * width + head]

            dve.wait_ge(s_tokens, blocks + 1)
            step(vec.memset(tok_diag, 0.0))
            step(vec.memset(attn_diag, 0.0))
            for q in range(pairs):
                step(vec.tensor_scalar(tok_rn[:, q:q + 1], ps_q[q][:, dim:dim + 1], NORM_EPS, None, ALU.add))
            step(vec.reciprocal(tok_rn, tok_rn))
            for q in range(pairs):
                step(vec.tensor_scalar(tokens[:, q, :], ps_q[q][:, 0:dim + 1], tok_rn[:, q:q + 1], None, ALU.mult))
            done()
            dve.wait_ge(s_c_pe, E_TT)
            step(vec.tensor_copy(tok_t0, ps_sum[0][:, :]))
            step(vec.tensor_copy(tok_t1, ps_sum[1][:, :]))
            step(vec.tensor_copy(norm_row, ps_tr[0:1, :]))
            done()
            dve.wait_ge(s_c_pe, E_TOK)
            for a in range(2):
                step(vec.tensor_copy(two(tok_diag, a, head), two(ps_x[:, :], a, head)))
            done()
            dve.wait_ge(s_c_pe, E_QKV)
            step(vec.tensor_copy(q_t, ps_sum[0][:, :]))
            step(vec.tensor_copy(k_t, ps_sum[1][:, :]))
            step(vec.tensor_copy(v_sb, ps_tr[:, :]))
            done()
            dve.wait_ge(s_c_pe, E_LOGITS)
            attn_q = attn[:, 0:pairs * head].rearrange("p (q n) -> p q n", q=pairs)
            for a in range(2):
                step(vec.tensor_scalar(attn_q[a * head:(a + 1) * head], two(ps_x[:, :], a, head), scale, None,
                                       ALU.mult))
            step(vec.tensor_reduce(attn_max, attn_q, AX_X, ALU.max))
            step(vec.tensor_tensor(attn_q, attn_q, attn_max.unsqueeze(2).to_broadcast([P, pairs, head]),
                                   ALU.subtract))
            done()
            dve.wait_ge(s_c_exp, 1)
            step(vec.tensor_reduce(attn_sum, attn_q, AX_X, ALU.add))
            step(vec.reciprocal(attn_sum, attn_sum))
            for a in range(2):
                part = slice(a * head, (a + 1) * head)
                step(vec.tensor_tensor(two(attn_diag, a, head), attn_q[part],
                                       attn_sum[part].unsqueeze(2).to_broadcast([head, pairs, head]), ALU.mult))
            done()
            dve.wait_ge(s_c_pe, E_ATTN_T)
            step(vec.tensor_copy(attn_t, ps_sum[0][:, :]))
            done()
            dve.wait_ge(s_c_pe, E_OS)
            step(vec.tensor_copy(os_t, ps_sum[1][:, :]))
            done()
            dve.wait_ge(s_c_pe, E_MIX)
            dve.wait_ge(s_stored[0], 16 * (blocks // 2 + blocks))
            step(vec.tensor_copy(mix[:, 0:2, :], ps_x[:, :].rearrange("p (q n) -> p q n", q=2)))
            step(vec.tensor_copy(mix[:, 2:4, :], ps_tr[:, :].rearrange("p (q n) -> p q n", q=2)))
            done()

            def add_residual(k, slot, uses):
                if not isinstance(uses, int) or uses:
                    dve.wait_ge(s_o_stored[slot], uses * 16)
                dve.wait_ge(s_o_mm, k + 1)
                vec.tensor_tensor(y_out[:, slot, :], ps_q[slot][:, 0:dim], res_at(k), ALU.add
                                  ).then_inc(s_o_sum, 1)

            for k in range(out_slots):
                add_residual(k, k, 0)
            with dve.Fori(0, (blocks - 2) // out_slots - 1) as i:
                for s in range(out_slots):
                    add_residual(i * out_slots + (out_slots + s), s, i + 1)
            for k in range(blocks - 2, blocks):
                add_residual(k, k % out_slots, k // out_slots)

        @block.tensor
        def _(pe):
            mm = nc.tensor.matmul
            for semaphore in (*s_used, s_g_mm, s_logits, s_tokens, s_w_tr):
                pe.sem_inc(semaphore, 1)

            def transpose_into(target, source, size=P):
                return nc.tensor.transpose(target, source, ident[0:size, 0:size])

            def transpose_block(source, m):
                if not isinstance(m, int) or m:
                    pe.wait_ge(s_tr_copied, m)
                for k in range(2):
                    last = transpose_into(ps_tr[:, k * P:(k + 1) * P], source[:, k * P:(k + 1) * P])
                last.then_inc(s_tr, 1)

            def table_bank(n, c, slot):
                if not isinstance(n, int) or n:
                    pe.wait_ge(s_tab_sum[c], n)
                for k in range(2):
                    last = mm(ps_q[c][:, :], x_t[:, slot, k * P:(k + 1) * P],
                              w_rel[:, k, c * bank:(c + 1) * bank], start=(k == 0), stop=(k == 1))
                last.then_inc(s_tab_mm[c], 1)

            pe.wait_ge(s_pool_const, 7)
            pe.wait_ge(s_small, 16 * 15)
            for k in range(2):
                for q in range(pairs):
                    transpose_into(ps_sum[k][:, q * P:(q + 1) * P], w_x_sb[:, k, q * P:(q + 1) * P])
            transpose_into(ps_tr[:, 0:pairs], b_x_rows, pairs).then_inc(s_fold_pe, 1)
            pe.wait_ge(s_fold_dve, 1)
            for k in range(2):
                for q in range(pairs):
                    mm(ps_q[k][:, q * P:(q + 1) * P], w_x_t[:, k, q * P:(q + 1) * P], diag_w[:, 0, :],
                       start=True, stop=True)
            for q in range(pairs):
                last = mm(ps_q[2][:, q * P:(q + 1) * P], b_x_wide[:, q * P:(q + 1) * P], diag_w[:, 0, :],
                          start=True, stop=True)
            last.then_inc(s_fold_pe, 1)

            pe.wait_ge(s_fold_dve, 2)
            pe.wait_ge(s_xn, 1)
            transpose_block(xn, 0)
            pe.wait_ge(s_w0, 32)

            def table1_block(n, s, last=False):
                pe.wait_ge(s_tr_copied, n + 1)
                for c in range(2):
                    table_bank(n, c, s)
                if not last:
                    pe.wait_ge(s_xn, n + 2)
                    transpose_block(xn, n + 1)
                for c in range(2, banks):
                    table_bank(n, c, s)

            for n in range(2):
                table1_block(n, n)
            with pe.Fori(1, blocks // 2 - 1) as i:
                for s in range(2):
                    table1_block(i * 2 + s, s)
            table1_block(blocks - 2, 0)
            table1_block(blocks - 1, 1, last=True)

            pe.wait_ge(s_spread, 1)
            pe.wait_ge(s_tr_copied, blocks)
            transpose_into(ps_tr[0:2, 0:P], spread[:, :]).then_inc(s_spread_pe, 1)
            pe.wait_ge(s_spread, 2)
            transpose_into(ps_tr[0:1, 0:2], worst[:, :], 2).then_inc(s_spread_pe, 1)
            pe.wait_ge(s_flag, 1)
            general = pe.value_load(flag[0:1, 0:1], min_val=0, max_val=1)

            def sum_half(h, i):
                pe.wait_ge(s_onehot[h], i + 1)
                pe.wait_ge(s_sum_free[h], i + 1)
                for j in range(half_quads):
                    q = h * half_quads + j
                    pe.wait_ge(s_gathered[q], (i + 1) * (16 * QUAD))
                    for u in range(QUAD):
                        t = j * QUAD + u
                        last = mm(ps_sum[h][:, 0:dim], onehot[:, h, t, :], messages[:, h * TILES + t, :],
                                  start=(t == 0), stop=(t == TILES - 1))
                    last.then_inc(s_used[q], 1)

            def table2_block(k):
                pe.wait_ge(s_h, k + 1)
                transpose_block(h_block, k + blocks)
                pe.wait_ge(s_tr_copied, k + (blocks + 1))
                for c in range(banks):
                    table_bank(k + blocks, c, 0)

            def clear_tokens():
                for q in range(pairs):
                    pe.wait_ge(s_tab_sum[q], 2 * blocks)
                    mm(ps_q[q][:, 0:dim + 1], zero_tile[:, 0:P], zero_tile[:, 0:dim + 1], start=True, stop=False)

            def softmax_block(k, last_block=False):
                pe.wait_ge(s_xn, k + (blocks + 1))
                transpose_block(xn2, k + 2 * blocks)
                pe.wait_ge(s_tr_copied, k + (2 * blocks + 1))
                pe.wait_ge(s_w_copied, k + 1)
                for c in range(2):
                    last = mm(ps_x[:, :], x_t[:, 0, c * P:(c + 1) * P], w_fold[:, c, :],
                              start=(c == 0), stop=(c == 1))
                last.then_inc(s_logits, 1)
                pe.wait_ge(s_slice_w, k + 1)
                for q in range(pairs):
                    last = mm(ps_q[q][:, 0:dim + 1], slice_w[:, q * P:(q + 1) * P], xn2[:, :],
                              start=False, stop=last_block)
                last.then_inc(s_tokens, 1)
                for q in range(pairs):
                    last = transpose_into(ps_x[:, q * P:(q + 1) * P], slice_w[:, q * P:(q + 1) * P])
                last.then_inc(s_w_tr, 1)

            pe.wait_ge(s_w1, 32)
            pe.wait_ge(s_zeros, 2)
            with pe.If(general == 0):
                with pe.Fori(0, iters) as k:
                    for h in range(HALVES):
                        sum_half(h, k)
                    table2_block(k)
                table2_block(blocks - 1)
                clear_tokens()
                with pe.Fori(0, iters) as k:
                    for h in range(HALVES):
                        sum_half(h, k + iters)
                    softmax_block(k)
                softmax_block(blocks - 1, last_block=True)
            with pe.Else():
                for layer in range(2):
                    with pe.Fori(0, groups) as g:
                        for j in range(half_quads):
                            pe.wait_ge(s_g_gathered[j], (g + (layer * groups + 1)) * (16 * QUAD))
                        hold(pe, s_held_pe)
                        with pe.Fori(0, blocks) as w:
                            n = (g + layer * groups) * blocks + w
                            pe.wait_ge(s_g_onehot, n + 1)
                            pe.wait_ge(s_g_added, n + 1)
                            for t in range(TILES):
                                last = mm(ps_sum[0][:, 0:dim], onehot[:, 0, t, :], messages[:, t, :],
                                          start=(t == 0), stop=(t == TILES - 1))
                            last.then_inc(s_g_mm, 1)
                    if layer == 0:
                        with pe.Fori(0, blocks) as k:
                            table2_block(k)
                        clear_tokens()
                    else:
                        with pe.Fori(0, blocks - 1) as k:
                            softmax_block(k)
                        softmax_block(blocks - 1, last_block=True)
            pe.nop()

            def part(tile, q):
                return tile[:, q * P:(q + 1) * P]

            pe.wait_ge(s_c_dve, C_TOKENS)
            for k in range(2):
                for q in range(pairs):
                    transpose_into(part(ps_sum[k], q), tokens[:, q, k * P:(k + 1) * P])
            for q in range(pairs):
                last = transpose_into(ps_tr[0:1, q * P:(q + 1) * P], tokens[:, q, dim:dim + 1])
            last.then_inc(s_c_pe, 1)
            pe.wait_ge(s_c_dve, C_TT)
            pe.wait_ge(s_w_copied, blocks + 1)
            pe.wait_ge(s_late, 48)
            for q in range(pairs):
                mm(part(ps_x, q), w_fx_sb[:, 0, q * P:(q + 1) * P], part(tok_t0, q), start=True, stop=False)
                mm(part(ps_x, q), w_fx_sb[:, 1, q * P:(q + 1) * P], part(tok_t1, q), start=False, stop=False)
                last = mm(part(ps_x, q), b_fx_row[0:1, q * P:(q + 1) * P], norm_row[0:1, q * P:(q + 1) * P],
                          start=False, stop=True)
            last.then_inc(s_c_pe, 1)
            pe.wait_ge(s_c_dve, C_DIAG)
            mm(ps_sum[0][:, :], diag_w[:, 1, :], tok_diag, start=True, stop=True)
            mm(ps_sum[1][:, :], diag_w[:, 2, :], tok_diag, start=True, stop=True)
            for q in range(pairs):
                last = mm(part(ps_tr, q), part(tok_diag, q), diag_w[:, 3, :], start=True, stop=True)
            last.then_inc(s_c_pe, 1)
            pe.wait_ge(s_c_dve, C_QKV)
            for q in range(pairs):
                last = mm(part(ps_x, q), part(q_t, q), part(k_t, q), start=True, stop=True)
            last.then_inc(s_c_pe, 1)
            pe.wait_ge(s_c_dve, C_ATTN)
            for q in range(pairs):
                last = transpose_into(part(ps_sum[0], q), part(attn_diag, q))
            last.then_inc(s_c_pe, 1)
            pe.wait_ge(s_c_dve, C_ATTN_T)
            for q in range(pairs):
                last = mm(part(ps_sum[1], q), part(v_sb, q), part(attn_t, q), start=True, stop=True)
            last.then_inc(s_c_pe, 1)
            pe.wait_ge(s_c_dve, C_OS)
            for q in range(pairs):
                target = (ps_x, ps_tr)[q // 2][:, (q % 2) * dim:(q % 2 + 1) * dim]
                last = mm(target, part(os_t, q), w_out_sb[:, q, :], start=True, stop=True)
            last.then_inc(s_c_pe, 1)
            pe.wait_ge(s_c_dve, C_MIX)

            def output_block(k, slot, uses):
                pe.wait_ge(s_wslot[slot], (uses + 1) * 16)
                if not isinstance(k, int) or k >= out_slots:
                    pe.wait_ge(s_o_sum, k - (out_slots - 1))
                for q in range(pairs):
                    last = mm(ps_q[slot][:, 0:dim], w_in[:, slot, q * P:(q + 1) * P], mix[:, q, :],
                              start=(q == 0), stop=(q == pairs - 1))
                last.then_inc(s_o_mm, 1)

            for k in range(out_slots):
                output_block(k, k, 0)
            with pe.Fori(0, (blocks - 2) // out_slots - 1) as i:
                for s in range(out_slots):
                    output_block(i * out_slots + (out_slots + s), s, i + 1)
            for k in range(blocks - 2, blocks):
                output_block(k, k % out_slots, k // out_slots)


_INS = ['x', 'src', 'dst', 'edge_type_8', 'L0_gnn_W0', 'L0_gnn_b0', 'L0_gnn_W1', 'L0_gnn_b1', 'L0_ffn_W_fx',
        'L0_ffn_b_fx', 'L0_ffn_W_x', 'L0_ffn_b_x', 'L0_ffn_W_slice', 'L0_ffn_b_slice', 'L0_ffn_W_q', 'L0_ffn_W_k',
        'L0_ffn_W_v', 'L0_ffn_W_out', 'L0_ffn_b_out', 'L0_ffn_temperature']


def kernel(**inputs):
    import numpy as _np
    import concourse.bacc as _bacc
    from concourse import mybir as _mybir
    from concourse.bass_utils import run_bass_kernel_spmd as _run

    nc = _bacc.Bacc("TRN2", target_bir_lowering=False, num_devices=1)
    arrays, args = {}, []
    for name in _INS:
        a = _np.ascontiguousarray(inputs[name])
        arrays[f"in_{name}"] = a
        args.append(nc.dram_tensor(f"in_{name}", a.shape, _mybir.dt.from_np(a.dtype), kind="ExternalInput").ap())
    out = nc.dram_tensor("out_0", inputs['x'].shape, _mybir.dt.float32, kind="ExternalOutput").ap()
    build_program(nc, *args, out)
    r = _run(nc, [arrays], core_ids=[0])
    return r.results[0]["out_0"]
```

```python
from collections import namedtuple
from contextlib import ExitStack, contextmanager

import concourse.bass as bass
from concourse import mybir

ALU = mybir.AluOpType
ACT = mybir.ActivationFunctionType
F32 = mybir.dt.float32
I32 = mybir.dt.int32
AX_C = mybir.AxisListType.C
AX_X = mybir.AxisListType.X

P = 128
OFFSET = 32
STEP = 64
TILES = 16
QUAD = 4
HALVES = 2
LN_EPS = 1e-5
NORM_EPS = 1e-5


class Chain:

    def __init__(self, engine, semaphore):
        self.engine, self.semaphore, self.base, self.steps = engine, semaphore, 0, 0

    def __call__(self, instruction):
        self.steps += 1
        instruction.then_inc(self.semaphore, 1)
        self.engine.wait_ge(self.semaphore, self.base + self.steps)

    @contextmanager
    def loop(self, count, steps):
        base, before = self.base, self.steps
        with self.engine.Fori(0, count) as i:
            self.base, self.steps = base + before + i * steps, 0
            yield i
            assert self.steps == steps, f"{self.steps} steps"
        self.base, self.steps = base, before + count * steps


def build_program(nc, x, src, dst, edge_type, w0, b0, w1, b1, w_fx, b_fx, w_x, b_x, w_slice, b_slice,
                  w_q, w_k, w_v, w_out, b_out, temperature, out):
    nodes, dim = x.shape
    edges = src.shape[0]
    rels = w0.shape[0]
    inner = w_fx.shape[1]
    head = w_q.shape[0]
    heads = inner // head
    pairs = inner // P
    scale = float(head) ** -0.5
    blocks = -(-(nodes + OFFSET) // P)
    group = TILES * P
    iters = -(-edges // (HALVES * group))
    groups = iters * HALVES
    full_groups = edges // group
    rest = edges - full_groups * group
    rest_tiles = rest // P
    tail_rows = nodes + OFFSET - (blocks - 1) * P
    row = rels * dim
    bank = 512
    banks = row // bank
    slots = HALVES * TILES
    quads = slots // QUAD
    half_quads = quads // HALVES
    last_tiles = (*range(rest_tiles), (half_quads - 1) * QUAD)
    last_in_quad = [sum(t // QUAD == j for t in last_tiles) for j in range(half_quads)]
    assert dim == 2 * P and full_groups == groups - 1 and rest % P and rest_tiles % QUAD
    assert blocks == iters + 1 and pairs == banks == 4 and head * 2 == P and blocks % 2 == 0

    ctx = ExitStack()
    with ctx:
        def sb(name, shape, dt=F32):
            return ctx.enter_context(nc.sbuf_tensor(name, shape, dt))

        def ps(name):
            return ctx.enter_context(nc.psum_tensor(name, [P, bank], F32))

        def sem(name):
            return ctx.enter_context(nc.semaphore(name))

        def gathered(j, h, layer):
            return layer * 16 * (QUAD - last_in_quad[j]) if h == HALVES - 1 else 0

        table1 = nc.dram_tensor("table1", [blocks * P * rels + rels, dim], F32).ap()
        table2 = nc.dram_tensor("table2", [blocks * P * rels + rels, dim], F32).ap()
        weights_dram = nc.dram_tensor("slice_weights_t", [blocks, P, inner], F32).ap()

        res = sb("res", [P, blocks, dim])
        edge_row = sb("edge_row", [P, (iters + 1) * slots], I32)
        edge_col = sb("edge_col", [P, (iters + 1) * slots])
        edge_dst = sb("edge_dst", [P, (iters + 1) * slots])
        rows_now = sb("rows_now", [P, HALVES, TILES], I32)
        messages = sb("messages", [P, slots, dim])
        onehot = sb("onehot", [P, HALVES, TILES, P])
        w_rel = sb("w_rel", [P, 2, row])
        bias0 = sb("bias0", [P, dim])
        bias1 = sb("bias1", [P, dim])
        table_out = sb("table_out", [P, 2, row])
        ident = sb("ident", [P, P])
        iota_i = sb("iota_i", [P, HALVES, P], I32)
        iota = sb("iota", [P, HALVES, P])
        group_base_i = sb("group_base_i", [P, groups], I32)
        group_base = sb("group_base", [P, groups])
        valid = sb("valid", [P, blocks])
        h_block = sb("h_block", [P, dim])
        carry = sb("carry", [P, dim])
        x_t = sb("x_t", [P, 2, dim])
        xn = sb("xn", [P, dim])
        stats = sb("stats", [P, 6])
        moments = sb("moments", [P, 2])
        std = sb("std", [P, 1])
        rstd = sb("rstd", [P, 1])
        newton = sb("newton", [P, 1])
        furthest = sb("furthest", [P, 1])
        worst = sb("worst", [1, 1])
        flag = sb("flag", [1, 1], I32)
        dst_now = sb("dst_now", [P, TILES])
        zero_tile = sb("zero_tile", [P, dim + 1])
        x2 = sb("x2", [P, dim])
        xn2 = sb("xn2", [P, dim + 1])
        bias_out = sb("bias_out", [P, dim])
        w_fold = sb("w_fold", [P, 2, inner])
        bias_fold = sb("bias_fold", [P, inner])
        temp = sb("temp", [P, heads])
        b_slice_all = sb("b_slice_all", [P, head])
        logits = sb("logits", [P, inner])
        slice_w = sb("slice_w", [P, inner])
        head_max = sb("head_max", [P, heads])
        head_sum = sb("head_sum", [P, heads])
        weights_t = sb("weights_t", [P, inner])
        w_fx_sb = sb("w_fx_sb", [P, 2, inner])
        b_fx_row = sb("b_fx_row", [1, inner])
        w_out_sb = sb("w_out_sb", [P, pairs, dim])
        diag_w = sb("diag_w", [P, 4, P])
        typ_i = messages[:, 0:13, :].rearrange("p a b -> p (a b)").bitcast(I32)
        distance = messages[:, 0:13, :].rearrange("p a b -> p (a b)")
        dst_i = messages[:, 13:26, :].rearrange("p a b -> p (a b)").bitcast(I32)
        b_x_rows = logits[0:pairs, 0:P]
        b_x_t = slice_w[:, 0:pairs]
        w_x_sb = table_out[:, 1, 0:2 * inner].rearrange("p (k n) -> p k n", k=2)
        w_x_t = table_out[:, 1, 2 * inner:4 * inner].rearrange("p (k n) -> p k n", k=2)
        b_x_wide = weights_t[:, :]
        mes = messages[:, :, :].rearrange("p t d -> p (t d)")
        tokens = mes[:, 0:pairs * (dim + 1)].rearrange("p (q n) -> p q n", q=pairs)

        def stage4(n):
            return mes[:, 1100 + n * inner:1100 + (n + 1) * inner]

        tok_t0, tok_t1, tok_diag, q_t, k_t, v_sb, attn, attn_diag, attn_t, os_t = (stage4(n) for n in range(10))
        norm_row = mes[0:1, 6300:6300 + inner]
        tok_rn = mes[:, 6900:6900 + pairs]
        attn_max = mes[:, 6904:6904 + pairs]
        attn_sum = mes[:, 6908:6908 + pairs]
        mix = table_out[:, 0, 0:pairs * dim].rearrange("p (q n) -> p q n", q=pairs)
        out_slots = 4
        w_in = w_rel[:, :, :].rearrange("p k n -> p (k n)")[:, 0:out_slots * inner].rearrange(
            "p (s n) -> p s n", s=out_slots)
        y_out = table_out[:, 1, 0:out_slots * dim].rearrange("p (s n) -> p s n", s=out_slots)

        ps_sum = [ps("ps_sum0"), ps("ps_sum1")]
        ps_tr = ps("ps_tr")
        ps_x = ps("ps_x")
        ps_q = [ps(f"ps_q{c}") for c in range(banks)]

        Ffn = namedtuple("Ffn", "x2 xn2 logits slice_w weights_t head_max head_sum "
                         "ps_logits ps_tr x_t_slot")
        spare = onehot[:, :, :, :].rearrange("p a t c -> p (a t c)")
        main = Ffn(x2[:, :], xn2[:, :], logits[:, :], slice_w[:, :], weights_t[:, :],
                   head_max[:, :], head_sum[:, :], ps_x, ps_tr, 0)
        side = Ffn(spare[:, 0:dim], spare[:, dim:2 * dim + 1], *(
            spare[:, n * inner:(n + 1) * inner] for n in range(2, 5)),
            spare[:, 5 * inner:5 * inner + heads], spare[:, 6 * inner:6 * inner + heads], ps_sum[0], ps_tr, 0)
        last_main = main._replace(ps_tr=ps_sum[1], x_t_slot=1)

        s_zero_rows = sem("s_zero_rows")
        s_x = [sem(f"s_x{n}") for n in range(4)]
        s_edges = sem("s_edges")
        s_bias0 = sem("s_bias0")
        s_small = sem("s_small")
        s_late = sem("s_late")
        s_w0 = [sem(f"s_w0_{c}") for c in range(banks)]
        s_w1 = sem("s_w1")
        s_wslot = [sem(f"s_wslot{s}") for s in range(out_slots)]
        s_pool_const = sem("s_pool_const")
        s_pads = sem("s_pads")
        s_const = sem("s_const")
        s_zeros = sem("s_zeros")
        s_diag_zero = sem("s_diag_zero")
        s_zero_row_stored = sem("s_zero_row_stored")
        s_fold_pe = sem("s_fold_pe")
        s_fold_dve = sem("s_fold_dve")
        s_pool_lists = sem("s_pool_lists")
        s_lists = sem("s_lists")
        s_furthest = sem("s_furthest")
        s_flag = sem("s_flag")
        s_var = sem("s_var")
        s_std = sem("s_std")
        s_xn = sem("s_xn")
        s_tr = sem("s_tr")
        s_tr_copied = sem("s_tr_copied")
        s_tab_mm = [sem(f"s_tab_mm{c}") for c in range(banks)]
        s_tab_sum = [sem(f"s_tab_sum{c}") for c in range(banks)]
        s_relu = sem("s_relu")
        s_stored = [sem("s_stored0"), sem("s_stored1")]
        s_rows = [sem("s_rows0"), sem("s_rows1")]
        s_onehot = [sem("s_onehot0"), sem("s_onehot1")]
        s_gathered = [sem(f"s_gathered{q}") for q in range(quads)]
        s_used = [sem(f"s_used{q}") for q in range(quads)]
        s_sum_free = [sem("s_sum_free0"), sem("s_sum_free1")]
        s_h = sem("s_h")
        s_g_rows = sem("s_g_rows")
        s_g_gathered = [sem(f"s_g_gathered{q}") for q in range(half_quads)]
        s_g_onehot = sem("s_g_onehot")
        s_g_mm = sem("s_g_mm")
        s_g_added = sem("s_g_added")
        s_g_clear = sem("s_g_clear")
        s_g_x = sem("s_g_x")
        s_logits = sem("s_logits")
        s_shifted = sem("s_shifted")
        s_exp = sem("s_exp")
        s_slice_w = sem("s_slice_w")
        s_tokens = sem("s_tokens")
        s_w_tr = sem("s_w_tr")
        s_w_copied = sem("s_w_copied")
        s_w_stored = sem("s_w_stored")
        s_w_free = sem("s_w_free")
        s_c_pe = sem("s_c_pe")
        s_c_dve = sem("s_c_dve")
        s_c_exp = sem("s_c_exp")
        s_o_mm = sem("s_o_mm")
        s_o_sum = sem("s_o_sum")
        s_o_stored = [sem(f"s_o_stored{s}") for s in range(out_slots)]
        s_held_dve = sem("s_held_dve")
        s_held_pool = sem("s_held_pool")
        s_held_pe = sem("s_held_pe")
        s_dve_a = sem("s_dve_a")
        s_dve_f = sem("s_dve_f")
        s_dve_g = sem("s_dve_g")
        s_dve_c = sem("s_dve_c")

        (C_TOKENS, C_TT, C_DIAG, C_QKV, C_SHIFTED, C_ATTN, C_ATTN_T, C_OS, C_MIX) = range(1, 10)
        (E_TT, E_TOK, E_QKV, E_LOGITS, E_ATTN_T, E_OS, E_MIX) = range(1, 8)

        def hold(engine, semaphore):
            engine.sem_inc(semaphore, 1)

        def at(tile, k, width):
            if isinstance(k, int):
                return tile[:, k * width:(k + 1) * width]
            return tile[:, bass.ds(k * width, width)]

        res_flat = res[:, :, :].rearrange("p k d -> p (k d)")

        def res_at(k):
            return at(res_flat, k, dim)

        def table_rows(table, k):
            view = table[0:blocks * P * rels, :].rearrange("(k p r) o -> k p (r o)", p=P, r=rels)
            return view[k] if isinstance(k, int) else view[bass.ds(k, 1)].rearrange("a p n -> (a p) n")

        block = ctx.enter_context(nc.Block())

        @block.sync
        def _(sp):
            sp.sem_inc(s_w_free, 1)

            def load_x_edges(semaphore):
                sp.dma_start(res[OFFSET:P, 0, :], x[0:P - OFFSET, :]).then_inc(semaphore, 16)
                sp.dma_start(res[0:tail_rows, blocks - 1, :], x[nodes - tail_rows:nodes, :]).then_inc(semaphore, 16)

            def load_x(first, last, semaphore):
                view = x[P - OFFSET:nodes - tail_rows, :].rearrange("(k p) d -> p k d", p=P)
                sp.dma_start(res[:, first:last, :], view[:, first - 1:last - 1, :]).then_inc(semaphore, 16)

            def load_w(w, semaphores):
                part = rels // banks
                for c in range(banks):
                    for k in range(2):
                        sp.dma_start(w_rel[:, k, c * bank:(c + 1) * bank].rearrange("p (r o) -> p r o", r=part),
                                     w[c * part:(c + 1) * part, k * P:(k + 1) * P, :].rearrange("r p o -> p r o")
                                     ).then_inc(semaphores[c], 16)

            def store_table(n, k, slot, table):
                sp.wait_ge(s_relu, (n + 1) * banks)
                sp.dma_start(table_rows(table, k), table_out[:, slot, :]).then_inc(s_stored[slot], 16)

            def store_table_halves(n, k, slot, table):
                for part in range(2):
                    sp.wait_ge(s_relu, n * banks + (part + 1) * banks // 2)
                    columns = slice(part * row // 2, (part + 1) * row // 2)
                    sp.dma_start(table_rows(table, k)[:, columns], table_out[:, slot, columns]
                                 ).then_inc(s_stored[slot], 16)

            def store_weights(k, weights=weights_t[:, :]):
                sp.wait_ge(s_w_copied, k + 2)
                view = weights_dram[k] if isinstance(k, int) else \
                    weights_dram[bass.ds(k, 1)].rearrange("a p n -> (a p) n")
                sp.dma_start(view, weights).then_inc(s_w_stored, 16)

            def free_weights(k):
                sp.wait_ge(s_w_stored, (k + 1) * 16)
                sp.sem_inc(s_w_free, 1)

            sp.wait_ge(s_zero_rows, 1)
            load_x_edges(s_x[0])
            load_x(1, 3, s_x[1])
            load_w(w0, s_w0)
            sp.dma_start(bias0[:, :], b0.unsqueeze(0).to_broadcast([P, dim])).then_inc(s_bias0, 16)
            load_x(3, 13, s_x[2])
            sp.wait_ge(s_zeros, 2)
            for table in (table1, table2):
                sp.dma_start(table[blocks * P * rels:, :], carry[0:rels, :]).then_inc(s_zero_row_stored, 16)
            sp.wait_ge(s_pads, 1)
            lists = ((edge_row, src), (typ_i, edge_type), (dst_i, dst))
            for tile, values in lists:
                start = full_groups * group
                first = full_groups * TILES
                sp.dma_start(tile[:, first:first + rest_tiles],
                             values[start:start + rest_tiles * P].rearrange("(p t) -> p t", t=rest_tiles)
                             ).then_inc(s_edges, 16)
                sp.dma_start(tile[0:rest % P, first + last_tiles[-1]:first + last_tiles[-1] + 1],
                             values[start + rest_tiles * P:edges].rearrange("(p t) -> p t", t=1)
                             ).then_inc(s_edges, 16)

            def load_edges(tile, values, first, last):
                view = tile[:, 0:groups * TILES].rearrange("p (g t) -> p g t", t=TILES)
                sp.dma_start(view[:, first:last, :],
                             values[first * group:last * group].rearrange("(g p t) -> p g t", p=P, t=TILES)
                             ).then_inc(s_edges, 16)

            for k in range(3):
                store_table(k, k, k % 2, table1)
                load_x(13 + 12 * k, 25 + 12 * k, s_x[3])
            half = full_groups // 2
            for n, (tile, values) in enumerate(lists):
                for first, last in ((0, half), (half, full_groups)):
                    k += 1
                    store_table(k, k, k % 2, table1)
                    load_edges(tile, values, first, last)
            store_table(9, 9, 1, table1)
            sp.dma_start(b_x_rows, b_x.rearrange("(q p) -> q p", p=P)).then_inc(s_small, 16)
            sp.dma_start(temp[:, :], temperature.rearrange("a h b c -> (a b c) h").to_broadcast([P, heads])
                         ).then_inc(s_small, 16)
            sp.dma_start(b_slice_all[:, :], b_slice.unsqueeze(0).to_broadcast([P, head])).then_inc(s_small, 16)
            sp.dma_start(bias1[:, :], b1.unsqueeze(0).to_broadcast([P, dim])).then_inc(s_small, 16)
            sp.dma_start(bias_out[:, :], b_out.unsqueeze(0).to_broadcast([P, dim])).then_inc(s_small, 16)
            sp.wait_ge(s_diag_zero, 1)
            for n, w in enumerate((w_slice, w_q, w_k, w_v)):
                for a in range(2):
                    sp.dma_start(diag_w[a * head:(a + 1) * head, n, a * head:(a + 1) * head], w
                                 ).then_inc(s_small, 16)
            sp.dma_start(w_fx_sb[:, :, :], w_fx.rearrange("(k p) n -> p k n", p=P)).then_inc(s_late, 16)
            sp.dma_start(b_fx_row[:, :], b_fx.unsqueeze(0)).then_inc(s_late, 16)
            sp.dma_start(w_out_sb[:, :, :], w_out.rearrange("(q p) n -> p q n", p=P)).then_inc(s_late, 16)
            with sp.Fori(5, blocks // 2 - 1) as i:
                for s in range(2):
                    store_table(i * 2 + s, i * 2 + s, s, table1)
            store_table(blocks - 2, blocks - 2, 0, table1)
            store_table_halves(blocks - 1, blocks - 1, 1, table1)
            sp.wait_ge(s_tab_mm[banks - 1], blocks)
            sp.wait_ge(s_stored[1], 16 * (blocks // 2 + 1))
            sp.dma_start(w_x_sb, w_x.rearrange("(k p) n -> p k n", p=P)).then_inc(s_small, 16)
            load_w(w1, [s_w1] * banks)
            sp.wait_ge(s_flag, 1)
            general = sp.value_load(flag[0:1, 0:1], min_val=0, max_val=1)
            with sp.If(general == 0):
                with sp.Fori(0, iters - 1) as k:
                    store_table(k + blocks, k, 0, table2)
                for s in range(2):
                    store_table_halves(2 * blocks - 2 + s, blocks - 2 + s, s, table2)
                with sp.Fori(0, iters - 1) as k:
                    store_weights(k)
                    free_weights(k)
                store_weights(blocks - 2, side.weights_t)
                store_weights(blocks - 1)
            with sp.Else():
                with sp.Fori(0, blocks) as k:
                    store_table(k + blocks, k, 0, table2)
                sp.wait_ge(s_g_clear, 1)
                load_x_edges(s_g_x)
                load_x(1, blocks - 1, s_g_x)
                with sp.Fori(0, blocks) as k:
                    store_weights(k)
                    free_weights(k)
            sp.nop()

            sp.wait_ge(s_w_stored, blocks * 16)
            def load_weights(k, slot):
                if not isinstance(k, int) or k >= out_slots:
                    sp.wait_ge(s_o_mm, k - (out_slots - 1))
                view = weights_dram[k] if isinstance(k, int) else \
                    weights_dram[bass.ds(k, 1)].rearrange("a p n -> (a p) n")
                sp.dma_start(w_in[:, slot, :], view).then_inc(s_wslot[slot], 16)

            for k in range(out_slots):
                load_weights(k, k)
            with sp.Fori(0, (blocks - 2) // out_slots - 1) as i:
                for s in range(out_slots):
                    load_weights(i * out_slots + (out_slots + s), s)
            for k in range(blocks - 2, blocks):
                load_weights(k, k % out_slots)

        @block.gpsimd
        def _(pool):
            pool.memset(ident[:, :], 0.0).then_inc(s_pool_const, 1)
            pool.memset(valid[:, :], 1.0).then_inc(s_pool_const, 1)
            pool.wait_ge(s_pool_const, 2)
            pool.affine_select(out=ident[:, :], in_=ident[:, :], compare_op=ALU.not_equal, fill=1.0,
                               base=0, pattern=[[-1, P]], channel_multiplier=1).then_inc(s_pool_const, 1)
            pool.affine_select(out=valid[:, 0:1], in_=valid[:, 0:1], compare_op=ALU.is_ge, fill=0.0,
                               base=-OFFSET, pattern=[[0, 1]], channel_multiplier=1).then_inc(s_pool_const, 1)
            pool.affine_select(out=valid[:, blocks - 1:blocks], in_=valid[:, blocks - 1:blocks],
                               compare_op=ALU.is_ge, fill=0.0, base=tail_rows - 1, pattern=[[0, 1]],
                               channel_multiplier=-1).then_inc(s_pool_const, 1)
            pool.iota(iota_i[:, 0, :], pattern=[[1, P]], base=0, channel_multiplier=0).then_inc(s_pool_const, 1)
            pool.iota(iota_i[:, 1, 0:STEP], pattern=[[1, STEP]], base=STEP, channel_multiplier=0
                      ).then_inc(s_pool_const, 1)
            pool.iota(iota_i[:, 1, STEP:P], pattern=[[1, STEP]], base=0, channel_multiplier=0
                      ).then_inc(s_pool_const, 1)
            pool.iota(group_base_i[:, :], pattern=[[STEP, groups]], base=0, channel_multiplier=0
                      ).then_inc(s_pool_const, 1)

            step = Chain(pool, s_pool_lists)
            real = slice(0, groups * TILES)
            wrap = slice(iters * slots, (iters + 1) * slots)
            pool.wait_ge(s_pool_const, 9)
            step(pool.tensor_copy(group_base[:, :], group_base_i[:, :]))
            pool.wait_ge(s_edges, 16 * 12)
            step(pool.tensor_scalar(edge_row[:, real], edge_row[:, real], rels, OFFSET * rels, ALU.mult, ALU.add))
            step(pool.tensor_tensor(edge_row[:, real], edge_row[:, real], typ_i[:, real], ALU.add))
            step(pool.tensor_scalar(edge_dst[:, real], dst_i[:, real], float(OFFSET), None, ALU.add))
            step(pool.tensor_tensor(edge_col[:, real].rearrange("p (g t) -> p g t", t=TILES),
                                    edge_dst[:, real].rearrange("p (g t) -> p g t", t=TILES),
                                    group_base[:, :].unsqueeze(2).to_broadcast([P, groups, TILES]), ALU.subtract))
            step(pool.tensor_copy(edge_row[:, wrap], edge_row[:, 0:slots]))
            step(pool.tensor_copy(edge_col[:, wrap], edge_col[:, 0:slots]))
            step(pool.tensor_scalar(distance[:, real], edge_col[:, real], (P - 1) / 2, None, ALU.subtract))
            step(pool.tensor_tensor(distance[:, real], distance[:, real], distance[:, real], ALU.mult))
            pool.sem_inc(s_lists, 1)
            pool.wait_ge(s_furthest, 1)
            step(pool.tensor_reduce(worst[:, :], furthest[:, :], AX_C, ALU.max))
            step(pool.tensor_scalar(flag[:, :], worst[:, :], ((P - 1) / 2) ** 2, None, ALU.is_gt))
            pool.sem_inc(s_flag, 1)

            def gather(table, slot, half, t, semaphore):
                pool.indirect_dma_start(
                    out=messages[:, slot, :], out_offset=None, in_=table,
                    in_offset=bass.IndirectOffsetOnAxis(ap=rows_now[:, half, t:t + 1], axis=0)
                ).then_inc(semaphore, 16)

            def gather_iteration(table, i, last=False):
                for h in range(HALVES):
                    pool.wait_ge(s_rows[h], i + 1)
                    tiles = last_tiles if last and h == HALVES - 1 else range(TILES)
                    for j in range(half_quads):
                        q = h * half_quads + j
                        pool.wait_ge(s_used[q], i + 1)
                        hold(pool, s_held_pool)
                        for t in range(j * QUAD, (j + 1) * QUAD):
                            if t in tiles:
                                gather(table, h * TILES + t, h, t, s_gathered[q])

            pool.wait_ge(s_flag, 1)
            general = pool.value_load(flag[0:1, 0:1], min_val=0, max_val=1)
            pool.wait_ge(s_zero_row_stored, 32)
            for s in range(2):
                pool.wait_ge(s_stored[s], 16 * (blocks // 2 + s))
            with pool.If(general == 0):
                with pool.Fori(0, iters - 1) as i:
                    gather_iteration(table1, i)
                gather_iteration(table1, iters - 1, last=True)
                pool.wait_ge(s_stored[0], 16 * (blocks // 2 + blocks))
                pool.wait_ge(s_stored[1], 16 * (blocks // 2 + 3))
                with pool.Fori(0, iters - 1) as i:
                    gather_iteration(table2, i + iters)
                gather_iteration(table2, 2 * iters - 1, last=True)
            with pool.Else():
                for layer, table in enumerate((table1, table2)):
                    if layer:
                        pool.wait_ge(s_stored[0], 16 * (blocks // 2 + blocks))
                    with pool.Fori(0, groups) as g:
                        pool.wait_ge(s_g_rows, g + (layer * groups + 1))
                        pool.wait_ge(s_g_mm, (g + layer * groups) * blocks + 1)
                        hold(pool, s_held_pool)
                        for t in range(TILES):
                            gather(table, t, 0, t, s_g_gathered[t // QUAD])
            pool.nop()

        @block.scalar
        def _(act):
            act.sem_inc(s_w_copied, 1)

            def root(m):
                act.wait_ge(s_var, m + 1)
                nc.scalar.activation(std[:, :], moments[:, 1:2], ACT.Sqrt).then_inc(s_std, 1)

            def copy_transposed(m, slot, source=ps_tr):
                act.wait_ge(s_tr, m + 1)
                nc.scalar.activation(x_t[:, slot, :], source[:, 0:dim], ACT.Copy).then_inc(s_tr_copied, 1)

            def relu(n, c, slot):
                act.wait_ge(s_tab_sum[c], n + 1)
                part = table_out[:, slot, c * bank:(c + 1) * bank]
                nc.scalar.activation(part, part, ACT.Relu).then_inc(s_relu, 1)

            def table_block(k):
                act.wait_ge(s_tab_mm[banks - 1], k + blocks)
                copy_transposed(k + blocks, 0)
                for c in range(banks):
                    relu(k + blocks, c, 0)

            def ffn_block(k):
                root(k + blocks)
                if isinstance(k, int) and k == 0:
                    act.wait_ge(s_tab_mm[banks - 1], 2 * blocks)
                act.wait_ge(s_logits, k + 1)
                copy_transposed(k + 2 * blocks, 0)
                exponentials(k, main)
                copy_weights(k, main, k)

            def exponentials(k, buffers):
                act.wait_ge(s_shifted, k + 1)
                nc.scalar.activation(buffers.logits, buffers.logits, ACT.Exp).then_inc(s_exp, 1)

            def copy_weights(k, buffers, stored):
                act.wait_ge(s_w_tr, k + 2)
                act.wait_ge(s_w_free, stored + 1)
                nc.scalar.activation(buffers.weights_t, buffers.ps_logits[:, :], ACT.Copy).then_inc(s_w_copied, 1)

            root(0)
            copy_transposed(0, 0)

            def table1_block(n, s, last=False):
                if not last:
                    root(n + 1)
                relu(n, 0, s)
                if not last:
                    if not isinstance(n, int) or n:
                        act.wait_ge(s_tab_mm[banks - 1], n)
                    copy_transposed(n + 1, 1 - s)
                for c in range(1, banks):
                    relu(n, c, s)

            for n in range(2):
                table1_block(n, n)
            with act.Fori(1, blocks // 2 - 1) as i:
                for s in range(2):
                    table1_block(i * 2 + s, s)
            table1_block(blocks - 2, 0)
            table1_block(blocks - 1, 1, last=True)

            act.wait_ge(s_flag, 1)
            general = act.value_load(flag[0:1, 0:1], min_val=0, max_val=1)
            with act.If(general == 0):
                with act.Fori(0, iters - 1) as k:
                    table_block(k)
                act.wait_ge(s_tab_mm[banks - 1], 2 * blocks - 2)
                copy_transposed(2 * blocks - 2, 0)
                copy_transposed(2 * blocks - 1, 1, ps_x)
                for s in range(2):
                    for c in range(banks):
                        relu(2 * blocks - 2 + s, c, s)
                act.wait_ge(s_tab_mm[banks - 1], 2 * blocks)
                with act.Fori(0, iters - 1) as k:
                    ffn_block(k)
                last_pair = ((blocks - 2, side), (blocks - 1, last_main))
                for k, _ in last_pair:
                    root(k + blocks)
                act.wait_ge(s_logits, blocks - 1)
                for k, buffers in last_pair:
                    copy_transposed(k + 2 * blocks, buffers.x_t_slot, buffers.ps_tr)
                for k, buffers in last_pair:
                    exponentials(k, buffers)
                for k, buffers in last_pair:
                    copy_weights(k, buffers, blocks - 2)
            with act.Else():
                with act.Fori(0, blocks) as k:
                    table_block(k)
                act.wait_ge(s_tab_mm[banks - 1], 2 * blocks)
                with act.Fori(0, blocks) as k:
                    ffn_block(k)
            act.nop()

            act.wait_ge(s_c_dve, C_SHIFTED)
            nc.scalar.activation(attn[:, 0:pairs * head], attn[:, 0:pairs * head], ACT.Exp).then_inc(s_c_exp, 1)

            def store_out(k, slot, semaphore):
                act.wait_ge(s_o_sum, k + 1)
                if isinstance(k, int) and k == 0:
                    act.dma_start(out[0:P - OFFSET, :], y_out[OFFSET:P, slot, :]).then_inc(semaphore, 16)
                elif isinstance(k, int) and k == blocks - 1:
                    act.dma_start(out[nodes - tail_rows:nodes, :], y_out[0:tail_rows, slot, :]
                                  ).then_inc(semaphore, 16)
                else:
                    view = out[P - OFFSET:nodes - tail_rows, :].rearrange("(k p) d -> k p d", p=P)
                    view = view[k - 1] if isinstance(k, int) else \
                        view[bass.ds(k - 1, 1)].rearrange("a p d -> (a p) d")
                    act.dma_start(view, y_out[:, slot, :]).then_inc(semaphore, 16)

            for k in range(out_slots):
                store_out(k, k, s_o_stored[k])
            with act.Fori(0, (blocks - 2) // out_slots - 1) as i:
                for s in range(out_slots):
                    store_out(i * out_slots + (out_slots + s), s, s_o_stored[s])
            for k in range(blocks - 2, blocks):
                store_out(k, k % out_slots, s_o_stored[k % out_slots])
            for s in range(out_slots):
                act.wait_ge(s_o_stored[s], 16 * len(range(s, blocks, out_slots)))

        @block.vector
        def _(dve):
            vec = nc.vector
            step = Chain(dve, s_dve_a)
            for semaphore in (*s_sum_free, s_g_added):
                dve.sem_inc(semaphore, 1)

            def layer_norm(source, target, m, free):
                step(vec.bn_stats(stats[:, :], source))
                hold(dve, s_held_dve)
                step(vec.bn_aggr(moments[:, :], stats[:, :]))
                vec.tensor_scalar(moments[:, 1:2], moments[:, 1:2], LN_EPS, None, ALU.add).then_inc(s_var, 1)
                dve.wait_ge(s_std, m + 1)
                step(vec.reciprocal(rstd[:, :], std[:, :]))
                step(vec.scalar_tensor_tensor(newton[:, :], rstd[:, :], moments[:, 1:2], rstd[:, :],
                                              ALU.mult, ALU.mult))
                step(vec.tensor_scalar(newton[:, :], newton[:, :], -0.5, 1.5, ALU.mult, ALU.add))
                step(vec.tensor_tensor(rstd[:, :], rstd[:, :], newton[:, :], ALU.mult))
                free()
                vec.tensor_scalar(target, source, moments[:, 0:1], rstd[:, :], ALU.subtract, ALU.mult
                                  ).then_inc(s_xn, 1)

            LN_STEPS = 6

            def add_bias(n, slot, bias, stores):
                if not isinstance(stores, int) or stores:
                    dve.wait_ge(s_stored[slot], stores * 16)
                for c in range(banks):
                    dve.wait_ge(s_tab_mm[c], n + 1)
                    vec.tensor_tensor(
                        table_out[:, slot, c * bank:(c + 1) * bank].rearrange("p (r o) -> p r o", o=dim),
                        ps_q[c][:, :].rearrange("p (r o) -> p r o", o=dim),
                        bias[:, :].unsqueeze(1).to_broadcast([P, bank // dim, dim]), ALU.add
                    ).then_inc(s_tab_sum[c], 1)

            vec.memset(res[:, 0, :], 0.0)
            vec.memset(res[:, blocks - 1, :], 0.0).then_inc(s_zero_rows, 1)
            pads = slice(full_groups * TILES, groups * TILES)
            vec.memset(edge_row[:, pads], blocks * P - OFFSET)
            vec.memset(typ_i[:, pads], 0)
            vec.memset(dst_i[:, pads], STEP * full_groups).then_inc(s_pads, 1)
            vec.memset(diag_w[:, :, :], 0.0).then_inc(s_diag_zero, 1)
            vec.memset(zero_tile[:, :], 0.0).then_inc(s_zeros, 1)
            vec.memset(carry[:, :], 0.0).then_inc(s_zeros, 1)

            dve.wait_ge(s_pool_const, 9)
            step(vec.tensor_copy(iota[:, :, :], iota_i[:, :, :]))
            dve.wait_ge(s_x[0], 32)
            layer_norm(res_at(0), xn[:, :], 0, lambda: None)
            dve.wait_ge(s_bias0, 16)

            def table1_block(n, slot, stores, last=False):
                if not last:
                    layer_norm(res_at(n + 1), xn[:, :], n + 1,
                               lambda: dve.wait_ge(s_tr, n + 1))
                add_bias(n, slot, bias0, stores)

            dve.wait_ge(s_x[1], 16)
            for n in range(2):
                table1_block(n, n % 2, n // 2)
            dve.wait_ge(s_x[2], 16)
            for n in range(2, 12):
                table1_block(n, n % 2, n // 2)
            dve.wait_ge(s_x[3], 48)
            with step.loop(blocks // 2 - 7, 2 * LN_STEPS) as i:
                for s in range(2):
                    table1_block(i * 2 + (12 + s), s, i + 6)
            dve.wait_ge(s_lists, 1)
            vec.tensor_reduce(furthest[:, :], distance[:, 0:groups * TILES], AX_X, ALU.max
                              ).then_inc(s_furthest, 1)
            table1_block(blocks - 2, 0, blocks // 2 - 1)
            table1_block(blocks - 1, 1, blocks // 2 - 1, last=True)

            def prepare(h, i, k):
                at_half = at(edge_col, k * HALVES + h, TILES)
                vec.tensor_copy(rows_now[:, h, :], at(edge_row, k * HALVES + h, TILES)).then_inc(s_rows[h], 1)
                vec.tensor_tensor(onehot[:, h, :, :], iota[:, h, :].unsqueeze(1).to_broadcast([P, TILES, P]),
                                  at_half.unsqueeze(2).to_broadcast([P, TILES, P]), ALU.is_equal
                                  ).then_inc(s_onehot[h], 1)

            dve.wait_ge(s_flag, 1)
            dve.wait_ge(s_zero_row_stored, 32)
            for h in range(HALVES):
                prepare(h, 0, 0)

            dve.wait_ge(s_small, 16 * 14)
            step(vec.tensor_scalar(temp[:, :], temp[:, :], 0.1, 5.0, ALU.max, ALU.min))
            step(vec.reciprocal(temp[:, :], temp[:, :]))
            dve.wait_ge(s_fold_pe, 1)
            vec.tensor_copy(w_x_t[:, 0, :], ps_sum[0][:, :])
            vec.tensor_copy(w_x_t[:, 1, :], ps_sum[1][:, :])
            step(vec.tensor_copy(b_x_t, ps_tr[:, 0:pairs]))
            vec.tensor_copy(b_x_wide.rearrange("p (q n) -> p q n", q=pairs),
                            b_x_t.unsqueeze(2).to_broadcast([P, pairs, P])).then_inc(s_fold_dve, 1)
            dve.wait_ge(s_fold_pe, 2)
            inv_temp = temp[:, :].unsqueeze(2).to_broadcast([P, heads, head])
            for k, source in enumerate((ps_q[0], ps_q[1])):
                vec.tensor_tensor(w_fold[:, k, :].rearrange("p (h g) -> p h g", h=heads),
                                  source[:, :].rearrange("p (h g) -> p h g", h=heads), inv_temp, ALU.mult)
            fold_heads = bias_fold[:, :].rearrange("p (h g) -> p h g", h=heads)
            step(vec.tensor_tensor(fold_heads, ps_q[2][:, :].rearrange("p (h g) -> p h g", h=heads),
                                   b_slice_all[:, :].unsqueeze(1).to_broadcast([P, heads, head]), ALU.add))
            vec.tensor_tensor(fold_heads, fold_heads, inv_temp, ALU.mult).then_inc(s_fold_dve, 1)

            def norm_block(k, sums, buffers=main, uses=None):
                uses = k if uses is None else uses
                if not isinstance(uses, int) or uses:
                    dve.wait_ge(s_tokens, uses + 1)
                    dve.wait_ge(s_w_tr, uses + 1)
                if sums is None:
                    step(vec.tensor_copy(buffers.x2, res_at(k)))
                else:
                    step(vec.tensor_tensor(buffers.x2, res_at(k), sums, ALU.add))
                step(vec.tensor_tensor(res_at(k), buffers.x2, bias_out[:, :], ALU.add))
                step(vec.tensor_copy(buffers.xn2[:, dim:dim + 1], at(valid, k, 1)))
                layer_norm(buffers.x2, buffers.xn2[:, 0:dim], k + blocks, lambda: None)

            def shift_logits(k, buffers=main):
                dve.wait_ge(s_logits, k + 2)
                step(vec.tensor_tensor(buffers.logits, buffers.ps_logits[:, :], bias_fold[:, :], ALU.add))
                by_head = buffers.logits.rearrange("p (h g) -> p h g", h=heads)
                step(vec.tensor_reduce(buffers.head_max, by_head, AX_X, ALU.max))
                vec.tensor_tensor(by_head, by_head, buffers.head_max.unsqueeze(2).to_broadcast([P, heads, head]),
                                  ALU.subtract).then_inc(s_shifted, 1)

            def normalise(k, buffers=main):
                by_head = buffers.logits.rearrange("p (h g) -> p h g", h=heads)
                dve.wait_ge(s_exp, k + 1)
                step(vec.tensor_reduce(buffers.head_sum, by_head, AX_X, ALU.add))
                step(vec.reciprocal(buffers.head_sum, buffers.head_sum))
                vec.tensor_tensor(buffers.slice_w.rearrange("p (h g) -> p h g", h=heads), by_head,
                                  buffers.head_sum.unsqueeze(2).to_broadcast([P, heads, head]), ALU.mult
                                  ).then_inc(s_slice_w, 1)

            SOFTMAX_STEPS = 7 + LN_STEPS
            dve.wait_ge(s_flag, 1)
            general = dve.value_load(flag[0:1, 0:1], min_val=0, max_val=1)
            with dve.If(general == 0):
                step = Chain(dve, s_dve_f)

                def combine_first(i):
                    last = half_quads - 1
                    dve.wait_ge(s_used[last], i + 2)
                    step(vec.tensor_tensor(h_block[:, :], ps_sum[0][:, 0:dim], carry[:, :], ALU.add))
                    dve.sem_inc(s_sum_free[0], 1)

                def combine_second(i, rest_of_sums):
                    dve.wait_ge(s_used[quads - 1], i + 2)
                    step(vec.tensor_tensor(h_block[STEP:P, :], h_block[STEP:P, :], ps_sum[1][STEP:P, 0:dim],
                                           ALU.add))
                    step(vec.tensor_copy(rest_of_sums[0:STEP, :], ps_sum[1][0:STEP, 0:dim]))
                    dve.sem_inc(s_sum_free[1], 1)

                COMBINE_STEPS = 3

                with step.loop(iters - 1, COMBINE_STEPS) as k:
                    dve.wait_ge(s_tr, k + blocks)
                    combine_first(k)
                    prepare(0, k + 1, k + 1)
                    combine_second(k, carry)
                    prepare(1, k + 1, k + 1)
                    dve.sem_inc(s_h, 1)
                    add_bias(k + blocks, 0, bias1, k + blocks // 2)
                dve.wait_ge(s_tr, 2 * blocks - 2)
                combine_first(iters - 1)
                prepare(0, iters, iters)
                step(vec.memset(xn[STEP:P, :], 0.0))
                combine_second(iters - 1, xn)
                dve.sem_inc(s_h, 2)
                for s in range(2):
                    add_bias(2 * blocks - 2 + s, s, bias1, (blocks // 2 + blocks - 2, blocks // 2 + 1)[s])
                prepare(1, iters, iters)
                step(vec.memset(carry[:, :], 0.0))
                combine_first(iters)
                prepare(0, iters + 1, 1)
                combine_second(iters, carry)
                prepare(1, iters + 1, 1)

                def ffn_beside_sums(k, last=False):
                    norm_block(k, h_block[:, :])
                    combine_first(k + (iters + 1))
                    if not last:
                        prepare(0, k + (iters + 2), k + 2)
                    shift_logits(k)
                    normalise(k)
                    combine_second(k + (iters + 1), carry)
                    if not last:
                        prepare(1, k + (iters + 2), k + 2)

                with step.loop(iters - 2, COMBINE_STEPS + SOFTMAX_STEPS) as k:
                    ffn_beside_sums(k)
                ffn_beside_sums(iters - 2, last=True)
                norm_block(blocks - 2, h_block[:, :], side, 0)
                norm_block(blocks - 1, carry[:, :], last_main, blocks - 2)
                for act_on in (shift_logits, normalise):
                    act_on(blocks - 2, side)
                    act_on(blocks - 1, last_main)
            with dve.Else():
                step = Chain(dve, s_dve_g)
                for layer in range(2):
                    if layer == 0:
                        dve.wait_ge(s_tr, blocks)
                        step(vec.memset(res[:, :, :], 0.0))
                    else:
                        step(vec.memset(res[:, 0, :], 0.0))
                        step(vec.memset(res[:, blocks - 1, :], 0.0))
                        dve.sem_inc(s_g_clear, 1)
                        dve.wait_ge(s_g_x, 48)
                    with step.loop(groups, 1 + 3 * blocks) as g:
                        done = (g + layer * groups) * blocks
                        dve.wait_ge(s_g_mm, done + 1)
                        vec.tensor_copy(rows_now[:, 0, :], at(edge_row, g, TILES)).then_inc(s_g_rows, 1)
                        step(vec.tensor_copy(dst_now[:, :], at(edge_dst, g, TILES)))
                        hold(dve, s_held_dve)
                        with step.loop(blocks, 3) as w:
                            step(vec.tensor_tensor(
                                onehot[:, 0, :, :], iota[:, 0, :].unsqueeze(1).to_broadcast([P, TILES, P]),
                                dst_now[:, :].unsqueeze(2).to_broadcast([P, TILES, P]), ALU.is_equal))
                            dve.sem_inc(s_g_onehot, 1)
                            step(vec.tensor_scalar(dst_now[:, :], dst_now[:, :], float(P), None, ALU.subtract))
                            dve.wait_ge(s_g_mm, done + w + 2)
                            step(vec.tensor_tensor(res_at(w), res_at(w), ps_sum[0][:, 0:dim], ALU.add))
                            dve.sem_inc(s_g_added, 1)
                    if layer == 0:
                        with step.loop(blocks, 1) as k:
                            dve.wait_ge(s_tr, k + blocks)
                            step(vec.tensor_copy(h_block[:, :], res_at(k)))
                            dve.sem_inc(s_h, 1)
                            add_bias(k + blocks, 0, bias1, k + blocks // 2)
                    else:
                        with step.loop(blocks, SOFTMAX_STEPS) as k:
                            norm_block(k, None)
                            shift_logits(k)
                            normalise(k)
            dve.nop()

            step = Chain(dve, s_dve_c)

            def done():
                dve.sem_inc(s_c_dve, 1)

            def two(tile, a, width):
                return tile.rearrange("p (q n) -> p q n", q=pairs)[a * head:(a + 1) * head, :,
                                                                   a * width:a * width + head]

            dve.wait_ge(s_tokens, blocks + 1)
            step(vec.memset(tok_diag, 0.0))
            step(vec.memset(attn_diag, 0.0))
            for q in range(pairs):
                step(vec.tensor_scalar(tok_rn[:, q:q + 1], ps_q[q][:, dim:dim + 1], NORM_EPS, None, ALU.add))
            step(vec.reciprocal(tok_rn, tok_rn))
            for q in range(pairs):
                step(vec.tensor_scalar(tokens[:, q, :], ps_q[q][:, 0:dim + 1], tok_rn[:, q:q + 1], None, ALU.mult))
            done()
            dve.wait_ge(s_c_pe, E_TT)
            step(vec.tensor_copy(tok_t0, ps_sum[0][:, :]))
            step(vec.tensor_copy(tok_t1, ps_sum[1][:, :]))
            step(vec.tensor_copy(norm_row, ps_tr[0:1, :]))
            done()
            dve.wait_ge(s_c_pe, E_TOK)
            for a in range(2):
                step(vec.tensor_copy(two(tok_diag, a, head), two(ps_x[:, :], a, head)))
            done()
            dve.wait_ge(s_c_pe, E_QKV)
            step(vec.tensor_copy(q_t, ps_sum[0][:, :]))
            step(vec.tensor_copy(k_t, ps_sum[1][:, :]))
            step(vec.tensor_copy(v_sb, ps_tr[:, :]))
            done()
            dve.wait_ge(s_c_pe, E_LOGITS)
            attn_q = attn[:, 0:pairs * head].rearrange("p (q n) -> p q n", q=pairs)
            for a in range(2):
                step(vec.tensor_scalar(attn_q[a * head:(a + 1) * head], two(ps_x[:, :], a, head), scale, None,
                                       ALU.mult))
            step(vec.tensor_reduce(attn_max, attn_q, AX_X, ALU.max))
            step(vec.tensor_tensor(attn_q, attn_q, attn_max.unsqueeze(2).to_broadcast([P, pairs, head]),
                                   ALU.subtract))
            done()
            dve.wait_ge(s_c_exp, 1)
            step(vec.tensor_reduce(attn_sum, attn_q, AX_X, ALU.add))
            step(vec.reciprocal(attn_sum, attn_sum))
            for a in range(2):
                part = slice(a * head, (a + 1) * head)
                step(vec.tensor_tensor(two(attn_diag, a, head), attn_q[part],
                                       attn_sum[part].unsqueeze(2).to_broadcast([head, pairs, head]), ALU.mult))
            done()
            dve.wait_ge(s_c_pe, E_ATTN_T)
            step(vec.tensor_copy(attn_t, ps_sum[0][:, :]))
            done()
            dve.wait_ge(s_c_pe, E_OS)
            step(vec.tensor_copy(os_t, ps_sum[1][:, :]))
            done()
            dve.wait_ge(s_c_pe, E_MIX)
            dve.wait_ge(s_stored[0], 16 * (blocks // 2 + blocks))
            step(vec.tensor_copy(mix[:, 0:2, :], ps_x[:, :].rearrange("p (q n) -> p q n", q=2)))
            step(vec.tensor_copy(mix[:, 2:4, :], ps_tr[:, :].rearrange("p (q n) -> p q n", q=2)))
            done()

            def add_residual(k, slot, uses):
                if not isinstance(uses, int) or uses:
                    dve.wait_ge(s_o_stored[slot], uses * 16)
                dve.wait_ge(s_o_mm, k + 1)
                vec.tensor_tensor(y_out[:, slot, :], ps_q[slot][:, 0:dim], res_at(k), ALU.add
                                  ).then_inc(s_o_sum, 1)

            for k in range(out_slots):
                add_residual(k, k, 0)
            with dve.Fori(0, (blocks - 2) // out_slots - 1) as i:
                for s in range(out_slots):
                    add_residual(i * out_slots + (out_slots + s), s, i + 1)
            for k in range(blocks - 2, blocks):
                add_residual(k, k % out_slots, k // out_slots)

        @block.tensor
        def _(pe):
            mm = nc.tensor.matmul
            for semaphore in (*s_used, s_g_mm, s_logits, s_tokens, s_w_tr):
                pe.sem_inc(semaphore, 1)

            def transpose_into(target, source, size=P):
                return nc.tensor.transpose(target, source, ident[0:size, 0:size])

            def transpose_block(source, m, target=ps_tr):
                if target is ps_tr and (not isinstance(m, int) or m):
                    pe.wait_ge(s_tr_copied, m)
                for k in range(2):
                    last = transpose_into(target[:, k * P:(k + 1) * P], source[:, k * P:(k + 1) * P])
                last.then_inc(s_tr, 1)

            def table_bank(n, c, slot):
                if not isinstance(n, int) or n:
                    pe.wait_ge(s_tab_sum[c], n)
                for k in range(2):
                    last = mm(ps_q[c][:, :], x_t[:, slot, k * P:(k + 1) * P],
                              w_rel[:, k, c * bank:(c + 1) * bank], start=(k == 0), stop=(k == 1))
                last.then_inc(s_tab_mm[c], 1)

            pe.wait_ge(s_pool_const, 9)
            pe.wait_ge(s_xn, 1)
            transpose_block(xn, 0)
            def table1_block(n, s, last=False):
                pe.wait_ge(s_tr_copied, n + 1)
                for c in range(2):
                    if isinstance(n, int) and n == 0:
                        pe.wait_ge(s_w0[c], 32)
                    table_bank(n, c, s)
                if not last:
                    pe.wait_ge(s_xn, n + 2)
                    transpose_block(xn, n + 1)
                for c in range(2, banks):
                    if isinstance(n, int) and n == 0:
                        pe.wait_ge(s_w0[c], 32)
                    table_bank(n, c, s)

            for n in range(2):
                table1_block(n, n)
            with pe.Fori(1, blocks // 2 - 1) as i:
                for s in range(2):
                    table1_block(i * 2 + s, s)
            table1_block(blocks - 2, 0)
            table1_block(blocks - 1, 1, last=True)

            pe.wait_ge(s_small, 16 * 14)
            for k in range(2):
                for q in range(pairs):
                    transpose_into(ps_sum[k][:, q * P:(q + 1) * P], w_x_sb[:, k, q * P:(q + 1) * P])
            transpose_into(ps_tr[:, 0:pairs], b_x_rows, pairs).then_inc(s_fold_pe, 1)
            pe.wait_ge(s_fold_dve, 1)
            for k in range(2):
                for q in range(pairs):
                    mm(ps_q[k][:, q * P:(q + 1) * P], w_x_t[:, k, q * P:(q + 1) * P], diag_w[:, 0, :],
                       start=True, stop=True)
            for q in range(pairs):
                last = mm(ps_q[2][:, q * P:(q + 1) * P], b_x_wide[:, q * P:(q + 1) * P], diag_w[:, 0, :],
                          start=True, stop=True)
            last.then_inc(s_fold_pe, 1)

            pe.wait_ge(s_fold_dve, 2)
            pe.wait_ge(s_flag, 1)
            general = pe.value_load(flag[0:1, 0:1], min_val=0, max_val=1)

            def sum_half(h, i, layer, tiles=range(TILES), between=lambda: None):
                pe.wait_ge(s_onehot[h], i + 1)
                pe.wait_ge(s_sum_free[h], i + 1)
                for j in range(half_quads):
                    if j == half_quads - 1:
                        between()
                    q = h * half_quads + j
                    short = gathered(j, h, layer + (len(tiles) < TILES))
                    pe.wait_ge(s_gathered[q], (i + 1) * (16 * QUAD) - short)
                    for t in range(j * QUAD, (j + 1) * QUAD):
                        if t in tiles:
                            last = mm(ps_sum[h][:, 0:dim], onehot[:, h, t, :], messages[:, h * TILES + t, :],
                                      start=(t == 0), stop=(t == tiles[-1]))
                    last.then_inc(s_used[q], 1)

            def table2_block(k):
                pe.wait_ge(s_h, k + 1)
                transpose_block(h_block, k + blocks)
                pe.wait_ge(s_tr_copied, k + (blocks + 1))
                for c in range(banks):
                    table_bank(k + blocks, c, 0)

            def clear_tokens():
                for q in range(pairs):
                    pe.wait_ge(s_tab_sum[q], 2 * blocks)
                    mm(ps_q[q][:, 0:dim + 1], zero_tile[:, 0:P], zero_tile[:, 0:dim + 1], start=True, stop=False)

            def transpose_norm(k, buffers=main):
                pe.wait_ge(s_xn, k + (blocks + 1))
                transpose_block(buffers.xn2, k + 2 * blocks, buffers.ps_tr)

            def slice_logits(k, buffers=main, copied=None):
                pe.wait_ge(s_tr_copied, k + (2 * blocks + 1))
                pe.wait_ge(s_w_copied, (k if copied is None else copied) + 1)
                for c in range(2):
                    last = mm(buffers.ps_logits[:, :], x_t[:, buffers.x_t_slot, c * P:(c + 1) * P],
                              w_fold[:, c, :], start=(c == 0), stop=(c == 1))
                last.then_inc(s_logits, 1)

            def use_weights(k, buffers=main, last_block=False):
                pe.wait_ge(s_slice_w, k + 1)
                for q in range(pairs):
                    last = mm(ps_q[q][:, 0:dim + 1], buffers.slice_w[:, q * P:(q + 1) * P], buffers.xn2,
                              start=False, stop=last_block)
                last.then_inc(s_tokens, 1)
                for q in range(pairs):
                    last = transpose_into(buffers.ps_logits[:, q * P:(q + 1) * P],
                                          buffers.slice_w[:, q * P:(q + 1) * P])
                last.then_inc(s_w_tr, 1)

            def softmax_block(k, last_block=False):
                transpose_norm(k)
                slice_logits(k)
                use_weights(k, last_block=last_block)

            pe.wait_ge(s_w1, 32 * banks)
            pe.wait_ge(s_zeros, 2)
            with pe.If(general == 0):
                with pe.Fori(0, iters - 1) as k:
                    for h in range(HALVES):
                        sum_half(h, k, 0)
                    table2_block(k)
                sum_half(0, iters - 1, 0)
                sum_half(1, iters - 1, 0, last_tiles)
                pe.wait_ge(s_h, blocks)
                transpose_block(h_block, 2 * blocks - 2)
                transpose_block(xn, 2 * blocks - 1, ps_x)
                for s in range(2):
                    pe.wait_ge(s_tr_copied, 2 * blocks - 1 + s)
                    for c in range(banks):
                        table_bank(2 * blocks - 2 + s, c, s)
                clear_tokens()
                for h in range(HALVES):
                    sum_half(h, iters, 1)

                def ffn_beside_sums(k, tiles=range(TILES)):
                    sum_half(0, k + (iters + 1), 1, between=lambda: transpose_norm(k))
                    slice_logits(k)
                    sum_half(1, k + (iters + 1), 1, tiles)
                    use_weights(k)

                with pe.Fori(0, iters - 2) as k:
                    ffn_beside_sums(k)
                ffn_beside_sums(iters - 2, last_tiles)
                transpose_norm(blocks - 2, side)
                slice_logits(blocks - 2, side, blocks - 2)
                transpose_norm(blocks - 1, last_main)
                slice_logits(blocks - 1, last_main, blocks - 2)
                use_weights(blocks - 2, side)
                use_weights(blocks - 1, last_main, last_block=True)
            with pe.Else():
                for layer in range(2):
                    with pe.Fori(0, groups) as g:
                        for j in range(half_quads):
                            pe.wait_ge(s_g_gathered[j], (g + (layer * groups + 1)) * (16 * QUAD))
                        hold(pe, s_held_pe)
                        with pe.Fori(0, blocks) as w:
                            n = (g + layer * groups) * blocks + w
                            pe.wait_ge(s_g_onehot, n + 1)
                            pe.wait_ge(s_g_added, n + 1)
                            for t in range(TILES):
                                last = mm(ps_sum[0][:, 0:dim], onehot[:, 0, t, :], messages[:, t, :],
                                          start=(t == 0), stop=(t == TILES - 1))
                            last.then_inc(s_g_mm, 1)
                    if layer == 0:
                        with pe.Fori(0, blocks) as k:
                            table2_block(k)
                        clear_tokens()
                    else:
                        with pe.Fori(0, blocks - 1) as k:
                            softmax_block(k)
                        softmax_block(blocks - 1, last_block=True)
            pe.nop()

            def part(tile, q):
                return tile[:, q * P:(q + 1) * P]

            pe.wait_ge(s_c_dve, C_TOKENS)
            pe.wait_ge(s_w_copied, blocks + 1)
            for k in range(2):
                for q in range(pairs):
                    transpose_into(part(ps_sum[k], q), tokens[:, q, k * P:(k + 1) * P])
            for q in range(pairs):
                last = transpose_into(ps_tr[0:1, q * P:(q + 1) * P], tokens[:, q, dim:dim + 1])
            last.then_inc(s_c_pe, 1)
            pe.wait_ge(s_c_dve, C_TT)
            pe.wait_ge(s_late, 48)
            for q in range(pairs):
                mm(part(ps_x, q), w_fx_sb[:, 0, q * P:(q + 1) * P], part(tok_t0, q), start=True, stop=False)
                mm(part(ps_x, q), w_fx_sb[:, 1, q * P:(q + 1) * P], part(tok_t1, q), start=False, stop=False)
                last = mm(part(ps_x, q), b_fx_row[0:1, q * P:(q + 1) * P], norm_row[0:1, q * P:(q + 1) * P],
                          start=False, stop=True)
            last.then_inc(s_c_pe, 1)
            pe.wait_ge(s_c_dve, C_DIAG)
            mm(ps_sum[0][:, :], diag_w[:, 1, :], tok_diag, start=True, stop=True)
            mm(ps_sum[1][:, :], diag_w[:, 2, :], tok_diag, start=True, stop=True)
            for q in range(pairs):
                last = mm(part(ps_tr, q), part(tok_diag, q), diag_w[:, 3, :], start=True, stop=True)
            last.then_inc(s_c_pe, 1)
            pe.wait_ge(s_c_dve, C_QKV)
            for q in range(pairs):
                last = mm(part(ps_x, q), part(q_t, q), part(k_t, q), start=True, stop=True)
            last.then_inc(s_c_pe, 1)
            pe.wait_ge(s_c_dve, C_ATTN)
            for q in range(pairs):
                last = transpose_into(part(ps_sum[0], q), part(attn_diag, q))
            last.then_inc(s_c_pe, 1)
            pe.wait_ge(s_c_dve, C_ATTN_T)
            for q in range(pairs):
                last = mm(part(ps_sum[1], q), part(v_sb, q), part(attn_t, q), start=True, stop=True)
            last.then_inc(s_c_pe, 1)
            pe.wait_ge(s_c_dve, C_OS)
            for q in range(pairs):
                target = (ps_x, ps_tr)[q // 2][:, (q % 2) * dim:(q % 2 + 1) * dim]
                last = mm(target, part(os_t, q), w_out_sb[:, q, :], start=True, stop=True)
            last.then_inc(s_c_pe, 1)
            pe.wait_ge(s_c_dve, C_MIX)

            def output_block(k, slot, uses):
                pe.wait_ge(s_wslot[slot], (uses + 1) * 16)
                if not isinstance(k, int) or k >= out_slots:
                    pe.wait_ge(s_o_sum, k - (out_slots - 1))
                for q in range(pairs):
                    last = mm(ps_q[slot][:, 0:dim], w_in[:, slot, q * P:(q + 1) * P], mix[:, q, :],
                              start=(q == 0), stop=(q == pairs - 1))
                last.then_inc(s_o_mm, 1)

            for k in range(out_slots):
                output_block(k, k, 0)
            with pe.Fori(0, (blocks - 2) // out_slots - 1) as i:
                for s in range(out_slots):
                    output_block(i * out_slots + (out_slots + s), s, i + 1)
            for k in range(blocks - 2, blocks):
                output_block(k, k % out_slots, k // out_slots)


_INS = ['x', 'src', 'dst', 'edge_type_8', 'L0_gnn_W0', 'L0_gnn_b0', 'L0_gnn_W1', 'L0_gnn_b1', 'L0_ffn_W_fx',
        'L0_ffn_b_fx', 'L0_ffn_W_x', 'L0_ffn_b_x', 'L0_ffn_W_slice', 'L0_ffn_b_slice', 'L0_ffn_W_q', 'L0_ffn_W_k',
        'L0_ffn_W_v', 'L0_ffn_W_out', 'L0_ffn_b_out', 'L0_ffn_temperature']


def kernel(**inputs):
    import numpy as _np
    import concourse.bacc as _bacc
    from concourse import mybir as _mybir
    from concourse.bass_utils import run_bass_kernel_spmd as _run

    nc = _bacc.Bacc("TRN2", target_bir_lowering=False, num_devices=1)
    arrays, args = {}, []
    for name in _INS:
        a = _np.ascontiguousarray(inputs[name])
        arrays[f"in_{name}"] = a
        args.append(nc.dram_tensor(f"in_{name}", a.shape, _mybir.dt.from_np(a.dtype), kind="ExternalInput").ap())
    out = nc.dram_tensor("out_0", inputs['x'].shape, _mybir.dt.float32, kind="ExternalOutput").ap()
    build_program(nc, *args, out)
    r = _run(nc, [arrays], core_ids=[0])
    return r.results[0]["out_0"]
```

```python
from collections import namedtuple
from contextlib import ExitStack, contextmanager

import concourse.bass as bass
from concourse import mybir

ALU = mybir.AluOpType
ACT = mybir.ActivationFunctionType
F32 = mybir.dt.float32
I32 = mybir.dt.int32
AX_C = mybir.AxisListType.C
AX_X = mybir.AxisListType.X

P = 128
OFFSET = 32
STEP = 64
TILES = 16
QUAD = 4
HALVES = 2
LN_EPS = 1e-5
NORM_EPS = 1e-5


class Chain:

    def __init__(self, engine, semaphore):
        self.engine, self.semaphore, self.base, self.steps = engine, semaphore, 0, 0

    def __call__(self, instruction):
        self.steps += 1
        instruction.then_inc(self.semaphore, 1)
        self.engine.wait_ge(self.semaphore, self.base + self.steps)

    @contextmanager
    def loop(self, count, steps):
        base, before = self.base, self.steps
        with self.engine.Fori(0, count) as i:
            self.base, self.steps = base + before + i * steps, 0
            yield i
            assert self.steps == steps, f"{self.steps} steps"
        self.base, self.steps = base, before + count * steps


def build_program(nc, x, src, dst, edge_type, w0, b0, w1, b1, w_fx, b_fx, w_x, b_x, w_slice, b_slice,
                  w_q, w_k, w_v, w_out, b_out, temperature, out):
    nodes, dim = x.shape
    edges = src.shape[0]
    rels = w0.shape[0]
    inner = w_fx.shape[1]
    head = w_q.shape[0]
    heads = inner // head
    pairs = inner // P
    scale = float(head) ** -0.5
    blocks = -(-(nodes + OFFSET) // P)
    group = TILES * P
    iters = -(-edges // (HALVES * group))
    groups = iters * HALVES
    full_groups = edges // group
    rest = edges - full_groups * group
    rest_tiles = rest // P
    tab_blocks = -(-nodes // P)
    early = P - OFFSET
    copies = 2 * tab_blocks
    stores1 = (tab_blocks // 2 + 2, tab_blocks // 2)
    stores_all = stores1[0] + tab_blocks + 1
    tail_rows = nodes + OFFSET - (blocks - 1) * P
    row = rels * dim
    bank = 512
    banks = row // bank
    slots = HALVES * TILES
    quads = slots // QUAD
    half_quads = quads // HALVES
    last_tiles = (*range(rest_tiles), (half_quads - 1) * QUAD)
    last_in_quad = [sum(t // QUAD == j for t in last_tiles) for j in range(half_quads)]
    assert dim == 2 * P and full_groups == groups - 1 and rest % P and rest_tiles % QUAD
    assert blocks == iters + 1 and tab_blocks == iters and blocks % 2 == 0 and tail_rows <= OFFSET
    assert pairs == banks == 4 and head * 2 == P

    ctx = ExitStack()
    with ctx:
        def sb(name, shape, dt=F32):
            return ctx.enter_context(nc.sbuf_tensor(name, shape, dt))

        def ps(name):
            return ctx.enter_context(nc.psum_tensor(name, [P, bank], F32))

        def sem(name):
            return ctx.enter_context(nc.semaphore(name))

        def gathered_less(j, h, layer):
            return layer * 16 * (QUAD - last_in_quad[j]) if h == HALVES - 1 else 0

        table1 = nc.dram_tensor("table1", [tab_blocks * P * rels + rels, dim], F32).ap()
        table2 = nc.dram_tensor("table2", [tab_blocks * P * rels + rels, dim], F32).ap()
        weights_dram = nc.dram_tensor("slice_weights_t", [blocks, P, inner], F32).ap()

        res = sb("res", [P, blocks, dim])
        edge_row = sb("edge_row", [P, (iters + 1) * slots], I32)
        edge_col = sb("edge_col", [P, (iters + 1) * slots])
        edge_dst = sb("edge_dst", [P, (iters + 1) * slots])
        rows_now = sb("rows_now", [P, HALVES, TILES], I32)
        messages = sb("messages", [P, slots, dim])
        onehot = sb("onehot", [P, HALVES, TILES, P])
        w_rel = sb("w_rel", [P, 2, row])
        bias0 = sb("bias0", [P, dim])
        bias1 = sb("bias1", [P, dim])
        table_out = sb("table_out", [P, 2, row])
        ident = sb("ident", [P, P])
        iota_i = sb("iota_i", [P, HALVES, P], I32)
        iota = sb("iota", [P, HALVES, P])
        group_base_i = sb("group_base_i", [P, groups], I32)
        group_base = sb("group_base", [P, groups])
        valid = sb("valid", [P, blocks])
        h_block = sb("h_block", [P, dim])
        carry = sb("carry", [P, dim])
        x_t = sb("x_t", [P, 2, dim])
        xn = sb("xn", [P, dim])
        stats = sb("stats", [P, 6])
        moments = sb("moments", [P, 2])
        std = sb("std", [P, 1])
        rstd = sb("rstd", [P, 1])
        newton = sb("newton", [P, 1])
        furthest = sb("furthest", [P, 1])
        worst = sb("worst", [1, 1])
        flag = sb("flag", [1, 1], I32)
        dst_now = sb("dst_now", [P, TILES])
        zero_tile = sb("zero_tile", [P, dim + 1])
        x2 = sb("x2", [P, dim])
        xn2 = sb("xn2", [P, dim + 1])
        bias_out = sb("bias_out", [P, dim])
        w_fold = sb("w_fold", [P, 2, inner])
        bias_fold = sb("bias_fold", [P, inner])
        temp = sb("temp", [P, heads])
        b_slice_all = sb("b_slice_all", [P, head])
        logits = sb("logits", [P, inner])
        slice_w = sb("slice_w", [P, inner])
        head_max = sb("head_max", [P, heads])
        head_sum = sb("head_sum", [P, heads])
        weights_t = sb("weights_t", [P, inner])
        w_fx_sb = sb("w_fx_sb", [P, 2, inner])
        b_fx_row = sb("b_fx_row", [1, inner])
        w_out_sb = sb("w_out_sb", [P, pairs, dim])
        diag_w = sb("diag_w", [P, 4, P])
        typ_i = messages[:, 0:13, :].rearrange("p a b -> p (a b)").bitcast(I32)
        distance = messages[:, 0:13, :].rearrange("p a b -> p (a b)")
        dst_i = messages[:, 13:26, :].rearrange("p a b -> p (a b)").bitcast(I32)
        b_x_rows = logits[0:pairs, 0:P]
        b_x_t = slice_w[:, 0:pairs]
        w_x_sb = table_out[:, 1, 0:2 * inner].rearrange("p (k n) -> p k n", k=2)
        w_x_t = table_out[:, 1, 2 * inner:4 * inner].rearrange("p (k n) -> p k n", k=2)
        b_x_wide = weights_t[:, :]
        mes = messages[:, :, :].rearrange("p t d -> p (t d)")
        tokens = mes[:, 0:pairs * (dim + 1)].rearrange("p (q n) -> p q n", q=pairs)

        def stage4(n):
            return mes[:, 1100 + n * inner:1100 + (n + 1) * inner]

        tok_t0, tok_t1, q_t, k_t, v_sb, attn, attn_t, os_t = (stage4(n) for n in range(8))
        norm_row = mes[0:1, 6300:6300 + inner]
        tok_rn = mes[:, 6900:6900 + pairs]
        attn_max = mes[:, 6904:6904 + pairs]
        attn_sum = mes[:, 6908:6908 + pairs]
        mix = table_out[:, 0, 0:pairs * dim].rearrange("p (q n) -> p q n", q=pairs)
        out_slots = 4
        w_in = w_rel[:, :, :].rearrange("p k n -> p (k n)")[:, 0:out_slots * inner].rearrange(
            "p (s n) -> p s n", s=out_slots)
        y_out = table_out[:, 1, 0:out_slots * dim].rearrange("p (s n) -> p s n", s=out_slots)
        diagonals = table_out[:, 1, row // 2:row // 2 + 2 * inner]
        tok_diag, attn_diag = diagonals[:, 0:inner], diagonals[:, inner:2 * inner]

        ps_sum = [ps("ps_sum0"), ps("ps_sum1")]
        ps_tr = ps("ps_tr")
        ps_x = ps("ps_x")
        ps_q = [ps(f"ps_q{c}") for c in range(banks)]

        Ffn = namedtuple("Ffn", "x2 xn2 logits slice_w weights_t head_max head_sum "
                         "ps_logits ps_tr x_t_slot")
        spare = onehot[:, :, :, :].rearrange("p a t c -> p (a t c)")
        main = Ffn(x2[:, :], xn2[:, :], logits[:, :], slice_w[:, :], weights_t[:, :],
                   head_max[:, :], head_sum[:, :], ps_x, ps_tr, 0)
        side = Ffn(spare[:, 0:dim], spare[:, dim:2 * dim + 1], *(
            spare[:, n * inner:(n + 1) * inner] for n in range(2, 5)),
            spare[:, 5 * inner:5 * inner + heads], spare[:, 6 * inner:6 * inner + heads], ps_sum[0], ps_tr, 0)
        last_main = main._replace(ps_tr=ps_sum[1], x_t_slot=1)

        s_zero_rows = sem("s_zero_rows")
        s_x = [sem(f"s_x{n}") for n in range(4)]
        s_edges = sem("s_edges")
        s_bias0 = sem("s_bias0")
        s_small = sem("s_small")
        s_late = sem("s_late")
        s_w0 = [sem(f"s_w0_{c}") for c in range(banks)]
        s_w1 = sem("s_w1")
        s_wslot = [sem(f"s_wslot{s}") for s in range(out_slots)]
        s_pool_const = sem("s_pool_const")
        s_pads = sem("s_pads")
        s_zeros = sem("s_zeros")
        s_diag_zero = sem("s_diag_zero")
        s_zero_row_stored = sem("s_zero_row_stored")
        s_fold_pe = sem("s_fold_pe")
        s_fold_dve = sem("s_fold_dve")
        s_pool_lists = sem("s_pool_lists")
        s_lists = sem("s_lists")
        s_furthest = sem("s_furthest")
        s_flag = sem("s_flag")
        s_var = sem("s_var")
        s_std = sem("s_std")
        s_xn = sem("s_xn")
        s_tr = sem("s_tr")
        s_tr_first = sem("s_tr_first")
        s_tr_copied = sem("s_tr_copied")
        s_tab_mm = [sem(f"s_tab_mm{c}") for c in range(banks)]
        s_tab_sum = [sem(f"s_tab_sum{c}") for c in range(banks)]
        s_relu = sem("s_relu")
        s_stored = [sem("s_stored0"), sem("s_stored1")]
        s_rows = [sem("s_rows0"), sem("s_rows1")]
        s_onehot = [sem("s_onehot0"), sem("s_onehot1")]
        s_gathered = [sem(f"s_gathered{q}") for q in range(quads)]
        s_used = [sem(f"s_used{q}") for q in range(quads)]
        s_sum_free = [sem("s_sum_free0"), sem("s_sum_free1")]
        s_h = sem("s_h")
        s_g_rows = sem("s_g_rows")
        s_g_gathered = [sem(f"s_g_gathered{q}") for q in range(half_quads)]
        s_g_onehot = sem("s_g_onehot")
        s_g_mm = sem("s_g_mm")
        s_g_added = sem("s_g_added")
        s_g_clear = sem("s_g_clear")
        s_g_x = sem("s_g_x")
        s_logits = sem("s_logits")
        s_shifted = sem("s_shifted")
        s_exp = sem("s_exp")
        s_slice_w = sem("s_slice_w")
        s_tokens = sem("s_tokens")
        s_w_tr = sem("s_w_tr")
        s_w_copied = sem("s_w_copied")
        s_w_stored = sem("s_w_stored")
        s_w_free = sem("s_w_free")
        s_c_pe = sem("s_c_pe")
        s_c_dve = sem("s_c_dve")
        s_c_act = sem("s_c_act")
        s_o_mm = sem("s_o_mm")
        s_o_sum = sem("s_o_sum")
        s_o_stored = [sem(f"s_o_stored{s}") for s in range(out_slots)]
        s_held_dve = sem("s_held_dve")
        s_held_pool = sem("s_held_pool")
        s_held_pe = sem("s_held_pe")
        s_dve_a = sem("s_dve_a")
        s_dve_f = sem("s_dve_f")
        s_dve_g = sem("s_dve_g")
        s_dve_c = sem("s_dve_c")

        (C_TOKENS, C_TT, C_DIAG, C_Q, C_SHIFTED, C_ATTN, C_ATTN_T, C_OS, C_MIX) = range(1, 10)
        (E_TT, E_TOK, E_QK, E_V, E_LOGITS, E_ATTN_T, E_OS, E_MIX) = range(1, 9)
        (A_TT, A_K, A_EXP, A_MIX) = range(1, 5)

        def hold(engine, semaphore):
            engine.sem_inc(semaphore, 1)

        def at(tile, k, width):
            if isinstance(k, int):
                return tile[:, k * width:(k + 1) * width]
            return tile[:, bass.ds(k * width, width)]

        res_flat = res[:, :, :].rearrange("p k d -> p (k d)")

        def res_at(k):
            return at(res_flat, k, dim)

        def table_rows(table, k):
            view = table[0:tab_blocks * P * rels, :].rearrange("(k p r) o -> k p (r o)", p=P, r=rels)
            return view[k] if isinstance(k, int) else view[bass.ds(k, 1)].rearrange("a p n -> (a p) n")

        block = ctx.enter_context(nc.Block())

        @block.sync
        def _(sp):
            sp.sem_inc(s_w_free, 1)

            def load_x_edges(semaphore):
                sp.dma_start(res[OFFSET:P, 0, :], x[0:P - OFFSET, :]).then_inc(semaphore, 16)
                sp.dma_start(res[0:tail_rows, blocks - 1, :], x[nodes - tail_rows:nodes, :]).then_inc(semaphore, 16)

            def load_x(first, last, semaphore):
                view = x[P - OFFSET:nodes - tail_rows, :].rearrange("(k p) d -> p k d", p=P)
                sp.dma_start(res[:, first:last, :], view[:, first - 1:last - 1, :]).then_inc(semaphore, 16)

            def load_w(w, semaphores):
                part = rels // banks
                for c in range(banks):
                    for k in range(2):
                        sp.dma_start(w_rel[:, k, c * bank:(c + 1) * bank].rearrange("p (r o) -> p r o", r=part),
                                     w[c * part:(c + 1) * part, k * P:(k + 1) * P, :].rearrange("r p o -> p r o")
                                     ).then_inc(semaphores[c], 16)

            def store_table(n, k, slot, table):
                sp.wait_ge(s_relu, (n + 1) * banks)
                sp.dma_start(table_rows(table, k), table_out[:, slot, :]).then_inc(s_stored[slot], 16)

            def store_table_halves(n, k, slot, table):
                for part in range(2):
                    sp.wait_ge(s_relu, n * banks + (part + 1) * banks // 2)
                    columns = slice(part * row // 2, (part + 1) * row // 2)
                    sp.dma_start(table_rows(table, k)[:, columns], table_out[:, slot, columns]
                                 ).then_inc(s_stored[slot], 16)

            def store_weights(k, weights=weights_t[:, :]):
                sp.wait_ge(s_w_copied, k + 2)
                view = weights_dram[k] if isinstance(k, int) else \
                    weights_dram[bass.ds(k, 1)].rearrange("a p n -> (a p) n")
                sp.dma_start(view, weights).then_inc(s_w_stored, 16)

            def free_weights(k):
                sp.wait_ge(s_w_stored, (k + 1) * 16)
                sp.sem_inc(s_w_free, 1)

            sp.wait_ge(s_zero_rows, 1)
            load_x_edges(s_x[0])
            load_x(1, 3, s_x[1])
            load_w(w0, s_w0)
            sp.dma_start(bias0[:, :], b0.unsqueeze(0).to_broadcast([P, dim])).then_inc(s_bias0, 16)
            load_x(3, 13, s_x[2])
            sp.wait_ge(s_zeros, 2)
            for table in (table1, table2):
                sp.dma_start(table[tab_blocks * P * rels:, :], carry[0:rels, :]).then_inc(s_zero_row_stored, 16)
            sp.wait_ge(s_pads, 1)
            lists = ((edge_row, src), (typ_i, edge_type), (dst_i, dst))
            for tile, values in lists:
                start = full_groups * group
                first = full_groups * TILES
                sp.dma_start(tile[:, first:first + rest_tiles],
                             values[start:start + rest_tiles * P].rearrange("(p t) -> p t", t=rest_tiles)
                             ).then_inc(s_edges, 16)
                sp.dma_start(tile[0:rest % P, first + last_tiles[-1]:first + last_tiles[-1] + 1],
                             values[start + rest_tiles * P:edges].rearrange("(p t) -> p t", t=1)
                             ).then_inc(s_edges, 16)

            def load_edges(tile, values, first, last):
                view = tile[:, 0:groups * TILES].rearrange("p (g t) -> p g t", t=TILES)
                sp.dma_start(view[:, first:last, :],
                             values[first * group:last * group].rearrange("(g p t) -> p g t", p=P, t=TILES)
                             ).then_inc(s_edges, 16)

            for n in range(3):
                store_table(n, n, n % 2, table1)
                load_x(13 + 12 * n, 25 + 12 * n, s_x[3])
            half = full_groups // 2
            pieces = [(*of, *piece) for of in lists for piece in ((0, half), (half, full_groups))]
            for n, piece in enumerate(pieces, 3):
                store_table(n, n, n % 2, table1)
                load_edges(*piece)
            store_table(9, 9, 1, table1)
            sp.dma_start(b_x_rows, b_x.rearrange("(q p) -> q p", p=P)).then_inc(s_small, 16)
            sp.dma_start(temp[:, :], temperature.rearrange("a h b c -> (a b c) h").to_broadcast([P, heads])
                         ).then_inc(s_small, 16)
            sp.dma_start(b_slice_all[:, :], b_slice.unsqueeze(0).to_broadcast([P, head])).then_inc(s_small, 16)
            sp.dma_start(bias1[:, :], b1.unsqueeze(0).to_broadcast([P, dim])).then_inc(s_small, 16)
            sp.dma_start(bias_out[:, :], b_out.unsqueeze(0).to_broadcast([P, dim])).then_inc(s_small, 16)
            sp.wait_ge(s_diag_zero, 1)
            for n, w in enumerate((w_slice, w_q, w_k, w_v)):
                for a in range(2):
                    sp.dma_start(diag_w[a * head:(a + 1) * head, n, a * head:(a + 1) * head], w
                                 ).then_inc(s_small, 16)
            sp.dma_start(w_fx_sb[:, :, :], w_fx.rearrange("(k p) n -> p k n", p=P)).then_inc(s_late, 16)
            sp.dma_start(b_fx_row[:, :], b_fx.unsqueeze(0)).then_inc(s_late, 16)
            sp.dma_start(w_out_sb[:, :, :], w_out.rearrange("(q p) n -> p q n", p=P)).then_inc(s_late, 16)
            with sp.Fori(5, tab_blocks // 2) as i:
                for s in range(2):
                    store_table(i * 2 + s, i * 2 + s, s, table1)
            store_table_halves(tab_blocks - 1, tab_blocks - 1, 0, table1)
            sp.wait_ge(s_tab_mm[banks - 1], tab_blocks)
            for s in range(2):
                sp.wait_ge(s_stored[s], 16 * stores1[s])
            sp.dma_start(w_x_sb, w_x.rearrange("(k p) n -> p k n", p=P)).then_inc(s_small, 16)
            load_w(w1, [s_w1] * banks)
            sp.wait_ge(s_flag, 1)
            general = sp.value_load(flag[0:1, 0:1], min_val=0, max_val=1)
            with sp.If(general == 0):
                with sp.Fori(0, tab_blocks - 1) as n:
                    store_table(n + tab_blocks, n, 0, table2)
                store_table_halves(2 * tab_blocks - 1, tab_blocks - 1, 0, table2)
                with sp.Fori(0, iters - 1) as k:
                    store_weights(k)
                    free_weights(k)
                store_weights(blocks - 2, side.weights_t)
                store_weights(blocks - 1)
            with sp.Else():
                with sp.Fori(0, tab_blocks - 1) as n:
                    store_table(n + tab_blocks, n, 0, table2)
                store_table_halves(2 * tab_blocks - 1, tab_blocks - 1, 0, table2)
                sp.wait_ge(s_g_clear, 1)
                load_x_edges(s_g_x)
                load_x(1, blocks - 1, s_g_x)
                with sp.Fori(0, blocks) as k:
                    store_weights(k)
                    free_weights(k)
            sp.nop()

            sp.wait_ge(s_w_stored, blocks * 16)
            def load_weights(k, slot):
                if not isinstance(k, int) or k >= out_slots:
                    sp.wait_ge(s_o_mm, k - (out_slots - 1))
                view = weights_dram[k] if isinstance(k, int) else \
                    weights_dram[bass.ds(k, 1)].rearrange("a p n -> (a p) n")
                sp.dma_start(w_in[:, slot, :], view).then_inc(s_wslot[slot], 16)

            for k in range(out_slots):
                load_weights(k, k)
            with sp.Fori(0, (blocks - 2) // out_slots - 1) as i:
                for s in range(out_slots):
                    load_weights(i * out_slots + (out_slots + s), s)
            for k in range(blocks - 2, blocks):
                load_weights(k, k % out_slots)

        @block.gpsimd
        def _(pool):
            pool.memset(ident[:, :], 0.0).then_inc(s_pool_const, 1)
            pool.memset(valid[:, :], 1.0).then_inc(s_pool_const, 1)
            pool.wait_ge(s_pool_const, 2)
            pool.affine_select(out=ident[:, :], in_=ident[:, :], compare_op=ALU.not_equal, fill=1.0,
                               base=0, pattern=[[-1, P]], channel_multiplier=1).then_inc(s_pool_const, 1)
            pool.affine_select(out=valid[:, 0:1], in_=valid[:, 0:1], compare_op=ALU.is_ge, fill=0.0,
                               base=-OFFSET, pattern=[[0, 1]], channel_multiplier=1).then_inc(s_pool_const, 1)
            pool.affine_select(out=valid[:, blocks - 1:blocks], in_=valid[:, blocks - 1:blocks],
                               compare_op=ALU.is_ge, fill=0.0, base=tail_rows - 1, pattern=[[0, 1]],
                               channel_multiplier=-1).then_inc(s_pool_const, 1)
            pool.iota(iota_i[:, 0, :], pattern=[[1, P]], base=0, channel_multiplier=0).then_inc(s_pool_const, 1)
            pool.iota(iota_i[:, 1, 0:STEP], pattern=[[1, STEP]], base=STEP, channel_multiplier=0
                      ).then_inc(s_pool_const, 1)
            pool.iota(iota_i[:, 1, STEP:P], pattern=[[1, STEP]], base=0, channel_multiplier=0
                      ).then_inc(s_pool_const, 1)
            pool.iota(group_base_i[:, :], pattern=[[STEP, groups]], base=0, channel_multiplier=0
                      ).then_inc(s_pool_const, 1)

            step = Chain(pool, s_pool_lists)
            real = slice(0, groups * TILES)
            wrap = slice(iters * slots, (iters + 1) * slots)
            pool.wait_ge(s_pool_const, 9)
            step(pool.tensor_copy(group_base[:, :], group_base_i[:, :]))
            pool.wait_ge(s_edges, 16 * 12)
            step(pool.tensor_scalar(edge_row[:, real], edge_row[:, real], rels, None, ALU.mult))
            step(pool.tensor_tensor(edge_row[:, real], edge_row[:, real], typ_i[:, real], ALU.add))
            step(pool.tensor_scalar(edge_dst[:, real], dst_i[:, real], float(OFFSET), None, ALU.add))
            step(pool.tensor_tensor(edge_col[:, real].rearrange("p (g t) -> p g t", t=TILES),
                                    edge_dst[:, real].rearrange("p (g t) -> p g t", t=TILES),
                                    group_base[:, :].unsqueeze(2).to_broadcast([P, groups, TILES]), ALU.subtract))
            step(pool.tensor_copy(edge_row[:, wrap], edge_row[:, 0:slots]))
            step(pool.tensor_copy(edge_col[:, wrap], edge_col[:, 0:slots]))
            step(pool.tensor_scalar(distance[:, real], edge_col[:, real], (P - 1) / 2, None, ALU.subtract))
            step(pool.tensor_tensor(distance[:, real], distance[:, real], distance[:, real], ALU.mult))
            pool.sem_inc(s_lists, 1)
            pool.wait_ge(s_furthest, 1)
            step(pool.tensor_reduce(worst[:, :], furthest[:, :], AX_C, ALU.max))
            step(pool.tensor_scalar(flag[:, :], worst[:, :], ((P - 1) / 2) ** 2, None, ALU.is_gt))
            pool.sem_inc(s_flag, 1)

            def gather(table, slot, half, t, semaphore):
                pool.indirect_dma_start(
                    out=messages[:, slot, :], out_offset=None, in_=table,
                    in_offset=bass.IndirectOffsetOnAxis(ap=rows_now[:, half, t:t + 1], axis=0)
                ).then_inc(semaphore, 16)

            def gather_iteration(table, i, last=False):
                for h in range(HALVES):
                    pool.wait_ge(s_rows[h], i + 1)
                    tiles = last_tiles if last and h == HALVES - 1 else range(TILES)
                    for j in range(half_quads):
                        q = h * half_quads + j
                        pool.wait_ge(s_used[q], i + 1)
                        hold(pool, s_held_pool)
                        for t in range(j * QUAD, (j + 1) * QUAD):
                            if t in tiles:
                                gather(table, h * TILES + t, h, t, s_gathered[q])

            pool.wait_ge(s_flag, 1)
            general = pool.value_load(flag[0:1, 0:1], min_val=0, max_val=1)
            pool.wait_ge(s_zero_row_stored, 32)
            for s in range(2):
                pool.wait_ge(s_stored[s], 16 * stores1[s])
            with pool.If(general == 0):
                with pool.Fori(0, iters - 1) as i:
                    gather_iteration(table1, i)
                gather_iteration(table1, iters - 1, last=True)
                pool.wait_ge(s_stored[0], 16 * stores_all)
                with pool.Fori(0, iters - 1) as i:
                    gather_iteration(table2, i + iters)
                gather_iteration(table2, 2 * iters - 1, last=True)
            with pool.Else():
                for layer, table in enumerate((table1, table2)):
                    if layer:
                        pool.wait_ge(s_stored[0], 16 * stores_all)
                    with pool.Fori(0, groups) as g:
                        pool.wait_ge(s_g_rows, g + (layer * groups + 1))
                        pool.wait_ge(s_g_mm, (g + layer * groups) * blocks + 1)
                        hold(pool, s_held_pool)
                        for t in range(TILES):
                            gather(table, t, 0, t, s_g_gathered[t // QUAD])
            pool.nop()

        @block.scalar
        def _(act):
            act.sem_inc(s_w_copied, 1)

            def root(m):
                act.wait_ge(s_var, m + 1)
                nc.scalar.activation(std[:, :], moments[:, 1:2], ACT.Sqrt).then_inc(s_std, 1)

            def copy_transposed(m, slot, source=ps_tr):
                act.wait_ge(s_tr, m + 1)
                nc.scalar.activation(x_t[:, slot, :], source[:, 0:dim], ACT.Copy).then_inc(s_tr_copied, 1)

            def copy_part(slot, rows, source_rows, source=ps_tr):
                nc.scalar.activation(x_t[:, slot, :].rearrange("p (k c) -> p k c", k=2)[:, :, rows],
                                     source[:, 0:dim].rearrange("p (k c) -> p k c", k=2)[:, :, source_rows],
                                     ACT.Copy).then_inc(s_tr_copied, 1)

            def copy_first_rows(slot, source=ps_tr):
                copy_part(slot, slice(early, P), slice(0, OFFSET), source)

            def copy_other_rows(slot):
                copy_part(slot, slice(0, early), slice(OFFSET, P))

            def relu(n, c, slot):
                act.wait_ge(s_tab_sum[c], n + 1)
                part = table_out[:, slot, c * bank:(c + 1) * bank]
                nc.scalar.activation(part, part, ACT.Relu).then_inc(s_relu, 1)

            def table_block(k, last=False):
                act.wait_ge(s_tr, k + (blocks + 1))
                copy_first_rows(0)
                n = k + (tab_blocks - 1)
                for c in range(banks - 1):
                    relu(n, c, 0)
                if not last:
                    act.wait_ge(s_tab_mm[banks - 1], n + 1)
                    copy_other_rows(0)
                relu(n, banks - 1, 0)

            def begin_table2():
                act.wait_ge(s_tr, blocks + 1)
                act.wait_ge(s_tab_mm[banks - 1], tab_blocks)
                copy_other_rows(0)

            def ffn_block(k):
                root(k + blocks)
                act.wait_ge(s_logits, k + 1)
                copy_transposed(k + 2 * blocks, 0)
                exponentials(k, main)
                copy_weights(k, main, k)

            def exponentials(k, buffers):
                act.wait_ge(s_shifted, k + 1)
                nc.scalar.activation(buffers.logits, buffers.logits, ACT.Exp).then_inc(s_exp, 1)

            def copy_weights(k, buffers, stored):
                act.wait_ge(s_w_tr, k + 2)
                act.wait_ge(s_w_free, stored + 1)
                nc.scalar.activation(buffers.weights_t, buffers.ps_logits[:, :], ACT.Copy).then_inc(s_w_copied, 1)

            root(0)
            act.wait_ge(s_tr, 1)
            copy_other_rows(0)
            root(1)
            act.wait_ge(s_tr, 2)
            copy_first_rows(0)
            copy_other_rows(1)

            def table1_block(n, s):
                if not isinstance(n, int) or n + 2 < blocks:
                    root(n + 2)
                relu(n, 0, s)
                if not isinstance(n, int) or n + 2 < blocks:
                    act.wait_ge(s_tr, n + 3)
                    copy_first_rows(1 - s)
                for c in range(1, banks - 1):
                    relu(n, c, s)
                if not isinstance(n, int) or n + 2 < tab_blocks:
                    act.wait_ge(s_tab_mm[banks - 1], n + 1)
                    copy_other_rows(s)
                relu(n, banks - 1, s)

            with act.Fori(0, tab_blocks // 2 - 1) as i:
                for s in range(2):
                    table1_block(i * 2 + s, s)
            for n in range(tab_blocks - 3, tab_blocks):
                table1_block(n, n % 2)

            act.wait_ge(s_flag, 1)
            general = act.value_load(flag[0:1, 0:1], min_val=0, max_val=1)
            with act.If(general == 0):
                begin_table2()

                def end_table_block(k):
                    act.wait_ge(s_tr_first, k)
                    copy_first_rows(0)
                    for c in range(banks):
                        relu(k + (tab_blocks - 1), c, 0)
                    act.wait_ge(s_tr, k + (blocks + 1))
                    act.wait_ge(s_tab_mm[banks - 1], k + tab_blocks)
                    copy_other_rows(0)

                with act.Fori(1, iters) as k:
                    end_table_block(k)
                act.wait_ge(s_tr, 2 * blocks)
                copy_first_rows(0, ps_x)
                for c in range(banks):
                    relu(2 * tab_blocks - 1, c, 0)
                act.wait_ge(s_tab_mm[banks - 1], 2 * tab_blocks)
                with act.Fori(0, iters - 1) as k:
                    ffn_block(k)
                last_pair = ((blocks - 2, side), (blocks - 1, last_main))
                for k, _ in last_pair:
                    root(k + blocks)
                act.wait_ge(s_logits, blocks - 1)
                for k, buffers in last_pair:
                    copy_transposed(k + 2 * blocks, buffers.x_t_slot, buffers.ps_tr)
                for k, buffers in last_pair:
                    exponentials(k, buffers)
                for k, buffers in last_pair:
                    copy_weights(k, buffers, blocks - 2)
            with act.Else():
                begin_table2()
                with act.Fori(1, blocks - 1) as k:
                    table_block(k)
                table_block(blocks - 1, last=True)
                act.wait_ge(s_tab_mm[banks - 1], 2 * tab_blocks)
                with act.Fori(0, blocks) as k:
                    ffn_block(k)
            act.nop()

            act.wait_ge(s_c_pe, E_TT)
            nc.scalar.activation(tok_t1, ps_sum[1][:, :], ACT.Copy).then_inc(s_c_act, 1)
            act.wait_ge(s_c_pe, E_QK)
            nc.scalar.activation(k_t, ps_sum[1][:, :], ACT.Copy).then_inc(s_c_act, 1)
            act.wait_ge(s_c_dve, C_SHIFTED)
            nc.scalar.activation(attn[:, 0:pairs * head], attn[:, 0:pairs * head], ACT.Exp, scale=scale
                                 ).then_inc(s_c_act, 1)
            act.wait_ge(s_c_pe, E_MIX)
            act.wait_ge(s_stored[0], 16 * stores_all)
            nc.scalar.activation(mix[:, 2:4, :], ps_tr[:, :].rearrange("p (q n) -> p q n", q=2), ACT.Copy
                                 ).then_inc(s_c_act, 1)

            def store_out(k, slot, semaphore):
                act.wait_ge(s_o_sum, k + 1)
                if isinstance(k, int) and k == 0:
                    act.dma_start(out[0:P - OFFSET, :], y_out[OFFSET:P, slot, :]).then_inc(semaphore, 16)
                elif isinstance(k, int) and k == blocks - 1:
                    act.dma_start(out[nodes - tail_rows:nodes, :], y_out[0:tail_rows, slot, :]
                                  ).then_inc(semaphore, 16)
                else:
                    view = out[P - OFFSET:nodes - tail_rows, :].rearrange("(k p) d -> k p d", p=P)
                    view = view[k - 1] if isinstance(k, int) else \
                        view[bass.ds(k - 1, 1)].rearrange("a p d -> (a p) d")
                    act.dma_start(view, y_out[:, slot, :]).then_inc(semaphore, 16)

            for k in range(out_slots):
                store_out(k, k, s_o_stored[k])
            with act.Fori(0, (blocks - 2) // out_slots - 1) as i:
                for s in range(out_slots):
                    store_out(i * out_slots + (out_slots + s), s, s_o_stored[s])
            for k in range(blocks - 2, blocks):
                store_out(k, k % out_slots, s_o_stored[k % out_slots])
            for s in range(out_slots):
                act.wait_ge(s_o_stored[s], 16 * len(range(s, blocks, out_slots)))

        @block.vector
        def _(dve):
            vec = nc.vector
            step = Chain(dve, s_dve_a)
            for semaphore in (*s_sum_free, s_g_added):
                dve.sem_inc(semaphore, 1)

            def layer_norm(source, target, m, free):
                step(vec.bn_stats(stats[:, :], source))
                hold(dve, s_held_dve)
                step(vec.bn_aggr(moments[:, :], stats[:, :]))
                vec.tensor_scalar(moments[:, 1:2], moments[:, 1:2], LN_EPS, None, ALU.add).then_inc(s_var, 1)
                dve.wait_ge(s_std, m + 1)
                step(vec.reciprocal(rstd[:, :], std[:, :]))
                step(vec.scalar_tensor_tensor(newton[:, :], rstd[:, :], moments[:, 1:2], rstd[:, :],
                                              ALU.mult, ALU.mult))
                step(vec.tensor_scalar(newton[:, :], newton[:, :], -0.5, 1.5, ALU.mult, ALU.add))
                step(vec.tensor_tensor(rstd[:, :], rstd[:, :], newton[:, :], ALU.mult))
                free()
                vec.tensor_scalar(target, source, moments[:, 0:1], rstd[:, :], ALU.subtract, ALU.mult
                                  ).then_inc(s_xn, 1)

            LN_STEPS = 6

            def add_bias(n, slot, bias, stores):
                if not isinstance(stores, int) or stores:
                    dve.wait_ge(s_stored[slot], stores * 16)
                for c in range(banks):
                    dve.wait_ge(s_tab_mm[c], n + 1)
                    vec.tensor_tensor(
                        table_out[:, slot, c * bank:(c + 1) * bank].rearrange("p (r o) -> p r o", o=dim),
                        ps_q[c][:, :].rearrange("p (r o) -> p r o", o=dim),
                        bias[:, :].unsqueeze(1).to_broadcast([P, bank // dim, dim]), ALU.add
                    ).then_inc(s_tab_sum[c], 1)

            vec.memset(res[:, 0, :], 0.0)
            vec.memset(res[:, blocks - 1, :], 0.0).then_inc(s_zero_rows, 1)
            pads = slice(full_groups * TILES, groups * TILES)
            vec.memset(edge_row[:, pads], tab_blocks * P)
            vec.memset(typ_i[:, pads], 0)
            vec.memset(dst_i[:, pads], STEP * full_groups).then_inc(s_pads, 1)
            vec.memset(diag_w[:, :, :], 0.0).then_inc(s_diag_zero, 1)
            vec.memset(zero_tile[:, :], 0.0).then_inc(s_zeros, 1)
            vec.memset(carry[:, :], 0.0).then_inc(s_zeros, 1)

            dve.wait_ge(s_pool_const, 9)
            step(vec.tensor_copy(iota[:, :, :], iota_i[:, :, :]))
            dve.wait_ge(s_x[0], 32)
            layer_norm(res_at(0), xn[:, :], 0, lambda: None)
            dve.wait_ge(s_x[1], 16)
            layer_norm(res_at(1), xn[:, :], 1, lambda: dve.wait_ge(s_tr, 1))
            dve.wait_ge(s_bias0, 16)

            def table1_block(n, slot, stores):
                if not isinstance(n, int) or n + 2 < blocks:
                    layer_norm(res_at(n + 2), xn[:, :], n + 2,
                               lambda: dve.wait_ge(s_tr, n + 2))
                add_bias(n, slot, bias0, stores)

            table1_block(0, 0, 0)
            dve.wait_ge(s_x[2], 16)
            for n in range(1, 10):
                table1_block(n, n % 2, n // 2)
            dve.wait_ge(s_x[3], 48)
            with step.loop(tab_blocks // 2 - 6, 2 * LN_STEPS) as i:
                for s in range(2):
                    table1_block(i * 2 + (10 + s), s, i + 5)
            dve.wait_ge(s_lists, 1)
            vec.tensor_reduce(furthest[:, :], distance[:, 0:groups * TILES], AX_X, ALU.max
                              ).then_inc(s_furthest, 1)
            for n in range(tab_blocks - 3, tab_blocks):
                table1_block(n, n % 2, n // 2)

            def prepare(h, i, k):
                at_half = at(edge_col, k * HALVES + h, TILES)
                vec.tensor_copy(rows_now[:, h, :], at(edge_row, k * HALVES + h, TILES)).then_inc(s_rows[h], 1)
                vec.tensor_tensor(onehot[:, h, :, :], iota[:, h, :].unsqueeze(1).to_broadcast([P, TILES, P]),
                                  at_half.unsqueeze(2).to_broadcast([P, TILES, P]), ALU.is_equal
                                  ).then_inc(s_onehot[h], 1)

            dve.wait_ge(s_flag, 1)
            dve.wait_ge(s_zero_row_stored, 32)
            for h in range(HALVES):
                prepare(h, 0, 0)

            dve.wait_ge(s_small, 16 * 14)
            step(vec.tensor_scalar(temp[:, :], temp[:, :], 0.1, 5.0, ALU.max, ALU.min))
            step(vec.reciprocal(temp[:, :], temp[:, :]))
            dve.wait_ge(s_fold_pe, 1)
            vec.tensor_copy(w_x_t[:, 0, :], ps_sum[0][:, :])
            vec.tensor_copy(w_x_t[:, 1, :], ps_sum[1][:, :])
            step(vec.tensor_copy(b_x_t, ps_tr[:, 0:pairs]))
            vec.tensor_copy(b_x_wide.rearrange("p (q n) -> p q n", q=pairs),
                            b_x_t.unsqueeze(2).to_broadcast([P, pairs, P])).then_inc(s_fold_dve, 1)
            dve.wait_ge(s_fold_pe, 2)
            inv_temp = temp[:, :].unsqueeze(2).to_broadcast([P, heads, head])
            for k, source in enumerate((ps_q[0], ps_q[1])):
                vec.tensor_tensor(w_fold[:, k, :].rearrange("p (h g) -> p h g", h=heads),
                                  source[:, :].rearrange("p (h g) -> p h g", h=heads), inv_temp, ALU.mult)
            fold_heads = bias_fold[:, :].rearrange("p (h g) -> p h g", h=heads)
            step(vec.tensor_tensor(fold_heads, ps_q[2][:, :].rearrange("p (h g) -> p h g", h=heads),
                                   b_slice_all[:, :].unsqueeze(1).to_broadcast([P, heads, head]), ALU.add))
            vec.tensor_tensor(fold_heads, fold_heads, inv_temp, ALU.mult).then_inc(s_fold_dve, 1)

            def norm_block(k, sums, buffers=main, uses=None):
                uses = k if uses is None else uses
                if not isinstance(uses, int) or uses:
                    dve.wait_ge(s_tokens, uses + 1)
                    dve.wait_ge(s_w_tr, uses + 1)
                if sums is None:
                    step(vec.tensor_copy(buffers.x2, res_at(k)))
                else:
                    step(vec.tensor_tensor(buffers.x2, res_at(k), sums, ALU.add))
                step(vec.tensor_tensor(res_at(k), buffers.x2, bias_out[:, :], ALU.add))
                step(vec.tensor_copy(buffers.xn2[:, dim:dim + 1], at(valid, k, 1)))
                layer_norm(buffers.x2, buffers.xn2[:, 0:dim], k + blocks, lambda: None)

            def shift_logits(k, buffers=main):
                dve.wait_ge(s_logits, k + 2)
                step(vec.tensor_tensor(buffers.logits, buffers.ps_logits[:, :], bias_fold[:, :], ALU.add))
                by_head = buffers.logits.rearrange("p (h g) -> p h g", h=heads)
                step(vec.tensor_reduce(buffers.head_max, by_head, AX_X, ALU.max))
                vec.tensor_tensor(by_head, by_head, buffers.head_max.unsqueeze(2).to_broadcast([P, heads, head]),
                                  ALU.subtract).then_inc(s_shifted, 1)

            def normalise(k, buffers=main):
                by_head = buffers.logits.rearrange("p (h g) -> p h g", h=heads)
                dve.wait_ge(s_exp, k + 1)
                step(vec.tensor_reduce(buffers.head_sum, by_head, AX_X, ALU.add))
                step(vec.reciprocal(buffers.head_sum, buffers.head_sum))
                vec.tensor_tensor(buffers.slice_w.rearrange("p (h g) -> p h g", h=heads), by_head,
                                  buffers.head_sum.unsqueeze(2).to_broadcast([P, heads, head]), ALU.mult
                                  ).then_inc(s_slice_w, 1)

            SOFTMAX_STEPS = 7 + LN_STEPS
            dve.wait_ge(s_flag, 1)
            general = dve.value_load(flag[0:1, 0:1], min_val=0, max_val=1)
            with dve.If(general == 0):
                step = Chain(dve, s_dve_f)

                def combine_first(i):
                    last = half_quads - 1
                    dve.wait_ge(s_used[last], i + 2)
                    step(vec.tensor_tensor(h_block[:, :], ps_sum[0][:, 0:dim], carry[:, :], ALU.add))
                    dve.sem_inc(s_sum_free[0], 1)

                def combine_second(i, rest_of_sums):
                    dve.wait_ge(s_used[quads - 1], i + 2)
                    step(vec.tensor_tensor(h_block[STEP:P, :], h_block[STEP:P, :], ps_sum[1][STEP:P, 0:dim],
                                           ALU.add))
                    step(vec.tensor_copy(rest_of_sums[0:STEP, :], ps_sum[1][0:STEP, 0:dim]))
                    dve.sem_inc(s_sum_free[1], 1)

                COMBINE_STEPS = 3

                combine_first(0)
                prepare(0, 1, 1)
                combine_second(0, carry)
                prepare(1, 1, 1)
                dve.sem_inc(s_h, 1)
                with step.loop(iters - 2, COMBINE_STEPS) as n:
                    dve.wait_ge(s_tr, n + (blocks + 1))
                    combine_first(n + 1)
                    dve.sem_inc(s_h, 1)
                    prepare(0, n + 2, n + 2)
                    add_bias(n + tab_blocks, 0, bias1, n + stores1[0])
                    dve.wait_ge(s_tr_first, n + 1)
                    combine_second(n + 1, carry)
                    dve.sem_inc(s_h, 1)
                    prepare(1, n + 2, n + 2)
                dve.wait_ge(s_tr, 2 * blocks - 2)
                combine_first(iters - 1)
                dve.sem_inc(s_h, 1)
                prepare(0, iters, iters)
                step(vec.memset(xn[STEP:P, :], 0.0))
                add_bias(2 * tab_blocks - 2, 0, bias1, stores_all - 3)
                dve.wait_ge(s_tr_first, iters - 1)
                combine_second(iters - 1, xn)
                dve.sem_inc(s_h, 1)
                add_bias(2 * tab_blocks - 1, 0, bias1, stores_all - 2)
                prepare(1, iters, iters)
                step(vec.memset(carry[:, :], 0.0))
                step(vec.memset(diagonals, 0.0))
                combine_first(iters)
                prepare(0, iters + 1, 1)
                combine_second(iters, carry)
                prepare(1, iters + 1, 1)

                def ffn_beside_sums(k, last=False):
                    norm_block(k, h_block[:, :])
                    combine_first(k + (iters + 1))
                    if not last:
                        prepare(0, k + (iters + 2), k + 2)
                    shift_logits(k)
                    normalise(k)
                    combine_second(k + (iters + 1), carry)
                    if not last:
                        prepare(1, k + (iters + 2), k + 2)

                with step.loop(iters - 2, COMBINE_STEPS + SOFTMAX_STEPS) as k:
                    ffn_beside_sums(k)
                ffn_beside_sums(iters - 2, last=True)
                norm_block(blocks - 2, h_block[:, :], side, 0)
                norm_block(blocks - 1, carry[:, :], last_main, blocks - 2)
                for act_on in (shift_logits, normalise):
                    act_on(blocks - 2, side)
                    act_on(blocks - 1, last_main)
            with dve.Else():
                step = Chain(dve, s_dve_g)
                for layer in range(2):
                    if layer == 0:
                        dve.wait_ge(s_tr, blocks)
                        step(vec.memset(res[:, :, :], 0.0))
                    else:
                        step(vec.memset(diagonals, 0.0))
                        step(vec.memset(res[:, 0, :], 0.0))
                        step(vec.memset(res[:, blocks - 1, :], 0.0))
                        dve.sem_inc(s_g_clear, 1)
                        dve.wait_ge(s_g_x, 48)
                    with step.loop(groups, 1 + 3 * blocks) as g:
                        done = (g + layer * groups) * blocks
                        dve.wait_ge(s_g_mm, done + 1)
                        vec.tensor_copy(rows_now[:, 0, :], at(edge_row, g, TILES)).then_inc(s_g_rows, 1)
                        step(vec.tensor_copy(dst_now[:, :], at(edge_dst, g, TILES)))
                        hold(dve, s_held_dve)
                        with step.loop(blocks, 3) as w:
                            step(vec.tensor_tensor(
                                onehot[:, 0, :, :], iota[:, 0, :].unsqueeze(1).to_broadcast([P, TILES, P]),
                                dst_now[:, :].unsqueeze(2).to_broadcast([P, TILES, P]), ALU.is_equal))
                            dve.sem_inc(s_g_onehot, 1)
                            step(vec.tensor_scalar(dst_now[:, :], dst_now[:, :], float(P), None, ALU.subtract))
                            dve.wait_ge(s_g_mm, done + w + 2)
                            step(vec.tensor_tensor(res_at(w), res_at(w), ps_sum[0][:, 0:dim], ALU.add))
                            dve.sem_inc(s_g_added, 1)
                    if layer == 0:
                        step(vec.tensor_copy(h_block[:, :], res_at(0)))
                        dve.sem_inc(s_h, 1)
                        with step.loop(tab_blocks, 1) as n:
                            dve.wait_ge(s_tr, n + (blocks + 1))
                            step(vec.tensor_copy(h_block[:, :], res_at(n + 1)))
                            dve.sem_inc(s_h, 1)
                            add_bias(n + tab_blocks, 0, bias1, n + stores1[0])
                    else:
                        with step.loop(blocks, SOFTMAX_STEPS) as k:
                            norm_block(k, None)
                            shift_logits(k)
                            normalise(k)
            dve.nop()

            step = Chain(dve, s_dve_c)

            def done():
                dve.sem_inc(s_c_dve, 1)

            def two(tile, a, width):
                return tile.rearrange("p (q n) -> p q n", q=pairs)[a * head:(a + 1) * head, :,
                                                                   a * width:a * width + head]

            dve.wait_ge(s_tokens, blocks + 1)
            for q in range(pairs):
                last = vec.tensor_scalar(tok_rn[:, q:q + 1], ps_q[q][:, dim:dim + 1], NORM_EPS, None, ALU.add)
            step(last)
            step(vec.reciprocal(tok_rn, tok_rn))
            for q in range(pairs):
                last = vec.tensor_scalar(tokens[:, q, :], ps_q[q][:, 0:dim + 1], tok_rn[:, q:q + 1], None, ALU.mult)
            step(last)
            done()
            dve.wait_ge(s_c_pe, E_TT)
            vec.tensor_copy(tok_t0, ps_sum[0][:, :])
            step(vec.tensor_copy(norm_row, ps_tr[0:1, :]))
            done()
            dve.wait_ge(s_c_pe, E_TOK)
            for a in range(2):
                last = vec.tensor_copy(two(tok_diag, a, head), two(ps_x[:, :], a, head))
            step(last)
            done()
            dve.wait_ge(s_c_pe, E_QK)
            step(vec.tensor_copy(q_t, ps_sum[0][:, :]))
            done()
            dve.wait_ge(s_c_pe, E_V)
            vec.tensor_copy(v_sb, ps_tr[:, :])
            dve.wait_ge(s_c_pe, E_LOGITS)
            attn_q = attn[:, 0:pairs * head].rearrange("p (q n) -> p q n", q=pairs)
            halves = [slice(a * head, (a + 1) * head) for a in range(2)]
            for a, part in enumerate(halves):
                last = vec.tensor_reduce(attn_max[part], two(ps_x[:, :], a, head), AX_X, ALU.max)
            step(last)
            for a, part in enumerate(halves):
                last = vec.tensor_tensor(attn_q[part], two(ps_x[:, :], a, head),
                                         attn_max[part].unsqueeze(2).to_broadcast([head, pairs, head]),
                                         ALU.subtract)
            step(last)
            done()
            dve.wait_ge(s_c_act, A_EXP)
            step(vec.tensor_reduce(attn_sum, attn_q, AX_X, ALU.add))
            step(vec.reciprocal(attn_sum, attn_sum))
            for a, part in enumerate(halves):
                last = vec.tensor_tensor(two(attn_diag, a, head), attn_q[part],
                                         attn_sum[part].unsqueeze(2).to_broadcast([head, pairs, head]), ALU.mult)
            step(last)
            done()
            dve.wait_ge(s_c_pe, E_ATTN_T)
            step(vec.tensor_copy(attn_t, ps_sum[0][:, :]))
            done()
            dve.wait_ge(s_c_pe, E_OS)
            step(vec.tensor_copy(os_t, ps_sum[1][:, :]))
            done()
            dve.wait_ge(s_c_pe, E_MIX)
            dve.wait_ge(s_stored[0], 16 * stores_all)
            step(vec.tensor_copy(mix[:, 0:2, :], ps_x[:, :].rearrange("p (q n) -> p q n", q=2)))
            done()

            def add_residual(k, slot, uses):
                if not isinstance(uses, int) or uses:
                    dve.wait_ge(s_o_stored[slot], uses * 16)
                dve.wait_ge(s_o_mm, k + 1)
                vec.tensor_tensor(y_out[:, slot, :], ps_q[slot][:, 0:dim], res_at(k), ALU.add
                                  ).then_inc(s_o_sum, 1)

            for k in range(out_slots):
                add_residual(k, k, 0)
            with dve.Fori(0, (blocks - 2) // out_slots - 1) as i:
                for s in range(out_slots):
                    add_residual(i * out_slots + (out_slots + s), s, i + 1)
            for k in range(blocks - 2, blocks):
                add_residual(k, k % out_slots, k // out_slots)

        @block.tensor
        def _(pe):
            mm = nc.tensor.matmul
            for semaphore in (*s_used, s_g_mm, s_logits, s_tokens, s_w_tr):
                pe.sem_inc(semaphore, 1)

            def transpose_into(target, source, size=P):
                return nc.tensor.transpose(target, source, ident[0:size, 0:size])

            def transpose_block(source, copied, target=ps_tr):
                if not isinstance(copied, int) or copied:
                    pe.wait_ge(s_tr_copied, copied)
                for k in range(2):
                    last = transpose_into(target[:, k * P:(k + 1) * P], source[:, k * P:(k + 1) * P])
                return last

            def table_bank(n, c, slot):
                if not isinstance(n, int) or n:
                    pe.wait_ge(s_tab_sum[c], n)
                for k in range(2):
                    last = mm(ps_q[c][:, :], x_t[:, slot, k * P:(k + 1) * P],
                              w_rel[:, k, c * bank:(c + 1) * bank], start=(k == 0), stop=(k == 1))
                last.then_inc(s_tab_mm[c], 1)

            pe.wait_ge(s_pool_const, 9)
            for m in range(2):
                pe.wait_ge(s_xn, m + 1)
                transpose_block(xn, m).then_inc(s_tr, 1)

            def table1_block(n, s):
                pe.wait_ge(s_tr_copied, n * 2 + 2)
                for c in range(banks):
                    if c == 2 and (not isinstance(n, int) or n + 2 < blocks):
                        pe.wait_ge(s_xn, n + 3)
                        transpose_block(xn, n * 2 + 3).then_inc(s_tr, 1)
                    if isinstance(n, int) and n == 0:
                        pe.wait_ge(s_w0[c], 32)
                    table_bank(n, c, s)

            for n in range(2):
                table1_block(n, n)
            with pe.Fori(1, tab_blocks // 2 - 1) as i:
                for s in range(2):
                    table1_block(i * 2 + s, s)
            for n in range(tab_blocks - 3, tab_blocks):
                table1_block(n, n % 2)

            pe.wait_ge(s_small, 16 * 14)
            for k in range(2):
                for q in range(pairs):
                    transpose_into(ps_sum[k][:, q * P:(q + 1) * P], w_x_sb[:, k, q * P:(q + 1) * P])
            transpose_into(ps_tr[:, 0:pairs], b_x_rows, pairs).then_inc(s_fold_pe, 1)
            pe.wait_ge(s_fold_dve, 1)
            for k in range(2):
                for q in range(pairs):
                    mm(ps_q[k][:, q * P:(q + 1) * P], w_x_t[:, k, q * P:(q + 1) * P], diag_w[:, 0, :],
                       start=True, stop=True)
            for q in range(pairs):
                last = mm(ps_q[2][:, q * P:(q + 1) * P], b_x_wide[:, q * P:(q + 1) * P], diag_w[:, 0, :],
                          start=True, stop=True)
            last.then_inc(s_fold_pe, 1)

            pe.wait_ge(s_fold_dve, 2)
            pe.wait_ge(s_flag, 1)
            general = pe.value_load(flag[0:1, 0:1], min_val=0, max_val=1)

            def sum_half(h, i, layer, tiles=range(TILES), ahead_of={}):
                pe.wait_ge(s_onehot[h], i + 1)
                pe.wait_ge(s_sum_free[h], i + 1)
                for j in range(half_quads):
                    if j in ahead_of:
                        ahead_of[j]()
                    q = h * half_quads + j
                    short = gathered_less(j, h, layer + (len(tiles) < TILES))
                    pe.wait_ge(s_gathered[q], (i + 1) * (16 * QUAD) - short)
                    for t in range(j * QUAD, (j + 1) * QUAD):
                        if t in tiles:
                            last = mm(ps_sum[h][:, 0:dim], onehot[:, h, t, :], messages[:, h * TILES + t, :],
                                      start=(t == 0), stop=(t == tiles[-1]))
                    last.then_inc(s_used[q], 1)

            def begin_table2():
                pe.wait_ge(s_h, 1)
                transpose_block(h_block, copies).then_inc(s_tr, 1)

            def end_table_block(k):
                pe.wait_ge(s_tr_copied, k * 2 + copies)
                for c in range(banks):
                    table_bank(k + (tab_blocks - 1), c, 0)

            def table2_block(k):
                pe.wait_ge(s_h, k + 1)
                transpose_block(h_block, k * 2 + (copies - 1)).then_inc(s_tr, 1)
                end_table_block(k)

            def clear_tokens():
                for q in range(pairs):
                    pe.wait_ge(s_tab_sum[q], 2 * tab_blocks)
                    mm(ps_q[q][:, 0:dim + 1], zero_tile[:, 0:P], zero_tile[:, 0:dim + 1], start=True, stop=False)

            def transpose_norm(k, buffers=main):
                pe.wait_ge(s_xn, k + (blocks + 1))
                copied = 2 * copies if buffers is last_main else k + 2 * copies
                transpose_block(buffers.xn2, copied, buffers.ps_tr).then_inc(s_tr, 1)

            def slice_logits(k, buffers=main, copied=None):
                pe.wait_ge(s_tr_copied, k + (2 * copies + 1))
                pe.wait_ge(s_w_copied, (k if copied is None else copied) + 1)
                for c in range(2):
                    last = mm(buffers.ps_logits[:, :], x_t[:, buffers.x_t_slot, c * P:(c + 1) * P],
                              w_fold[:, c, :], start=(c == 0), stop=(c == 1))
                last.then_inc(s_logits, 1)

            def use_weights(k, buffers=main, last_block=False):
                pe.wait_ge(s_slice_w, k + 1)
                for q in range(pairs):
                    last = mm(ps_q[q][:, 0:dim + 1], buffers.slice_w[:, q * P:(q + 1) * P], buffers.xn2,
                              start=False, stop=last_block)
                last.then_inc(s_tokens, 1)
                for q in range(pairs):
                    last = transpose_into(buffers.ps_logits[:, q * P:(q + 1) * P],
                                          buffers.slice_w[:, q * P:(q + 1) * P])
                last.then_inc(s_w_tr, 1)

            def softmax_block(k, last_block=False):
                transpose_norm(k)
                slice_logits(k)
                use_weights(k, last_block=last_block)

            pe.wait_ge(s_w1, 32 * banks)
            pe.wait_ge(s_zeros, 2)
            with pe.If(general == 0):
                for h in range(HALVES):
                    sum_half(h, 0, 0)
                begin_table2()

                def transpose_first_rows(k):
                    pe.wait_ge(s_h, k * 2)
                    transpose_block(h_block, k * 2 + (copies - 1)).then_inc(s_tr_first, 1)

                def sum_block(k, tiles=range(TILES)):
                    sum_half(0, k, 0)
                    sum_half(1, k, 0, tiles, {1: lambda: transpose_first_rows(k), 2: lambda: end_table_block(k)})
                    pe.wait_ge(s_h, k * 2 + 1)
                    transpose_block(h_block, k * 2 + copies).then_inc(s_tr, 1)

                with pe.Fori(1, iters - 1) as k:
                    sum_block(k)
                sum_block(iters - 1, last_tiles)
                transpose_block(xn, 2 * copies - 2, ps_x).then_inc(s_tr, 1)
                pe.wait_ge(s_tr_copied, 2 * copies)
                for c in range(banks):
                    table_bank(2 * tab_blocks - 1, c, 0)
                clear_tokens()
                for h in range(HALVES):
                    sum_half(h, iters, 1)

                def ffn_beside_sums(k, tiles=range(TILES)):
                    sum_half(0, k + (iters + 1), 1, ahead_of={half_quads - 1: lambda: transpose_norm(k)})
                    slice_logits(k)
                    sum_half(1, k + (iters + 1), 1, tiles)
                    use_weights(k)

                with pe.Fori(0, iters - 2) as k:
                    ffn_beside_sums(k)
                ffn_beside_sums(iters - 2, last_tiles)
                transpose_norm(blocks - 2, side)
                slice_logits(blocks - 2, side, blocks - 2)
                transpose_norm(blocks - 1, last_main)
                slice_logits(blocks - 1, last_main, blocks - 2)
                use_weights(blocks - 2, side)
                use_weights(blocks - 1, last_main, last_block=True)
            with pe.Else():
                for layer in range(2):
                    with pe.Fori(0, groups) as g:
                        for j in range(half_quads):
                            pe.wait_ge(s_g_gathered[j], (g + (layer * groups + 1)) * (16 * QUAD))
                        hold(pe, s_held_pe)
                        with pe.Fori(0, blocks) as w:
                            n = (g + layer * groups) * blocks + w
                            pe.wait_ge(s_g_onehot, n + 1)
                            pe.wait_ge(s_g_added, n + 1)
                            for t in range(TILES):
                                last = mm(ps_sum[0][:, 0:dim], onehot[:, 0, t, :], messages[:, t, :],
                                          start=(t == 0), stop=(t == TILES - 1))
                            last.then_inc(s_g_mm, 1)
                    if layer == 0:
                        begin_table2()
                        with pe.Fori(1, blocks) as k:
                            table2_block(k)
                        clear_tokens()
                    else:
                        with pe.Fori(0, blocks - 1) as k:
                            softmax_block(k)
                        softmax_block(blocks - 1, last_block=True)
            pe.nop()

            def part(tile, q):
                return tile[:, q * P:(q + 1) * P]

            pe.wait_ge(s_c_dve, C_TOKENS)
            pe.wait_ge(s_w_copied, blocks + 1)
            for k in range(2):
                for q in range(pairs):
                    transpose_into(part(ps_sum[k], q), tokens[:, q, k * P:(k + 1) * P])
            for q in range(pairs):
                last = transpose_into(ps_tr[0:1, q * P:(q + 1) * P], tokens[:, q, dim:dim + 1])
            last.then_inc(s_c_pe, 1)
            pe.wait_ge(s_c_dve, C_TT)
            pe.wait_ge(s_c_act, A_TT)
            pe.wait_ge(s_late, 48)
            for q in range(pairs):
                mm(part(ps_x, q), w_fx_sb[:, 0, q * P:(q + 1) * P], part(tok_t0, q), start=True, stop=False)
                mm(part(ps_x, q), w_fx_sb[:, 1, q * P:(q + 1) * P], part(tok_t1, q), start=False, stop=False)
                last = mm(part(ps_x, q), b_fx_row[0:1, q * P:(q + 1) * P], norm_row[0:1, q * P:(q + 1) * P],
                          start=False, stop=True)
            last.then_inc(s_c_pe, 1)
            pe.wait_ge(s_c_dve, C_DIAG)
            mm(ps_sum[0][:, :], diag_w[:, 1, :], tok_diag, start=True, stop=True)
            mm(ps_sum[1][:, :], diag_w[:, 2, :], tok_diag, start=True, stop=True).then_inc(s_c_pe, 1)
            for q in range(pairs):
                last = mm(part(ps_tr, q), part(tok_diag, q), diag_w[:, 3, :], start=True, stop=True)
            last.then_inc(s_c_pe, 1)
            pe.wait_ge(s_c_dve, C_Q)
            pe.wait_ge(s_c_act, A_K)
            for q in range(pairs):
                last = mm(part(ps_x, q), part(q_t, q), part(k_t, q), start=True, stop=True)
            last.then_inc(s_c_pe, 1)
            pe.wait_ge(s_c_dve, C_ATTN)
            for q in range(pairs):
                last = transpose_into(part(ps_sum[0], q), part(attn_diag, q))
            last.then_inc(s_c_pe, 1)
            pe.wait_ge(s_c_dve, C_ATTN_T)
            for q in range(pairs):
                last = mm(part(ps_sum[1], q), part(v_sb, q), part(attn_t, q), start=True, stop=True)
            last.then_inc(s_c_pe, 1)
            pe.wait_ge(s_c_dve, C_OS)
            for q in range(pairs):
                target = (ps_x, ps_tr)[q // 2][:, (q % 2) * dim:(q % 2 + 1) * dim]
                last = mm(target, part(os_t, q), w_out_sb[:, q, :], start=True, stop=True)
            last.then_inc(s_c_pe, 1)
            pe.wait_ge(s_c_dve, C_MIX)
            pe.wait_ge(s_c_act, A_MIX)

            def output_block(k, slot, uses):
                pe.wait_ge(s_wslot[slot], (uses + 1) * 16)
                if not isinstance(k, int) or k >= out_slots:
                    pe.wait_ge(s_o_sum, k - (out_slots - 1))
                for q in range(pairs):
                    last = mm(ps_q[slot][:, 0:dim], w_in[:, slot, q * P:(q + 1) * P], mix[:, q, :],
                              start=(q == 0), stop=(q == pairs - 1))
                last.then_inc(s_o_mm, 1)

            for k in range(out_slots):
                output_block(k, k, 0)
            with pe.Fori(0, (blocks - 2) // out_slots - 1) as i:
                for s in range(out_slots):
                    output_block(i * out_slots + (out_slots + s), s, i + 1)
            for k in range(blocks - 2, blocks):
                output_block(k, k % out_slots, k // out_slots)


_INS = ['x', 'src', 'dst', 'edge_type_8', 'L0_gnn_W0', 'L0_gnn_b0', 'L0_gnn_W1', 'L0_gnn_b1', 'L0_ffn_W_fx',
        'L0_ffn_b_fx', 'L0_ffn_W_x', 'L0_ffn_b_x', 'L0_ffn_W_slice', 'L0_ffn_b_slice', 'L0_ffn_W_q', 'L0_ffn_W_k',
        'L0_ffn_W_v', 'L0_ffn_W_out', 'L0_ffn_b_out', 'L0_ffn_temperature']


def kernel(**inputs):
    import numpy as _np
    import concourse.bacc as _bacc
    from concourse import mybir as _mybir
    from concourse.bass_utils import run_bass_kernel_spmd as _run

    nc = _bacc.Bacc("TRN2", target_bir_lowering=False, num_devices=1)
    arrays, args = {}, []
    for name in _INS:
        a = _np.ascontiguousarray(inputs[name])
        arrays[f"in_{name}"] = a
        args.append(nc.dram_tensor(f"in_{name}", a.shape, _mybir.dt.from_np(a.dtype), kind="ExternalInput").ap())
    out = nc.dram_tensor("out_0", inputs['x'].shape, _mybir.dt.float32, kind="ExternalOutput").ap()
    build_program(nc, *args, out)
    r = _run(nc, [arrays], core_ids=[0])
    return r.results[0]["out_0"]
```
